# Optimizing a Trainium2 kernel written in Bass

```python
import numpy as np
import jax
import jax.numpy as jnp

def _softmax(x, axis=-1):
    return jax.nn.softmax(x, axis=axis)

def _gelu(x):
    return jax.nn.gelu(x, approximate=True)

def _silu(x):
    return jax.nn.silu(x)

def _sigmoid(x):
    return jax.nn.sigmoid(x)

def _layernorm(x, axis=-1, eps=1e-05):
    m = jnp.mean(x, axis=axis, keepdims=True)
    v = jnp.var(x, axis=axis, keepdims=True)
    return (x - m) / jnp.sqrt(v + eps)

def _scatter_add(tgt, idx, src, axis=0):
    return tgt.at[idx].add(src)

def _segment_sum(src, seg, n):
    return jax.ops.segment_sum(src, seg, n)
kernel_name = 'mk_adj_preln_d4_adj_r2_e38b14'

def setup_inputs(seed: int=0):
    np.random.seed(seed)
    _w = jnp.asarray

    def _rec_inputs():
        import jax
        import jax.numpy as jnp
        _gk = jax.random.key(seed)
        x = -0.0001538 + 1 * jax.random.normal(jax.random.fold_in(_gk, 1), (64, 128, 384), jnp.float32)
        _w = (1.0 + jnp.arange(128, dtype=jnp.float32)) ** (-0.5)
        _w = _w / _w.mean()
        _pij = jnp.clip(0.03125 * _w[:, None] * _w[None, :], 0.0, 1.0)
        _a = jax.random.uniform(jax.random.fold_in(_gk, 2), (64, 128, 128)) < _pij
        _a = jnp.logical_or(_a, jnp.swapaxes(_a, -1, -2))
        _a = jnp.logical_or(_a, jnp.eye(128, dtype=bool))
        _af = _a.astype(jnp.float32)
        _af = _af * jax.random.uniform(jax.random.fold_in(_gk, 3), (64, 128, 128), jnp.float32, 0.05, 4.42607)
        adj = _af
        return (x, adj)
    x, adj = _rec_inputs()

    def _L0_gnn_setup():
        import jax, jax.numpy as jnp
        import numpy as np
        NUM_HEADS = 12
        HIDDEN = 384
        HEAD = HIDDEN // NUM_HEADS
        B, N = (16, 256)
        key = jax.random.key(seed)
        ks = jax.random.split(key, 9)
        s = 0.02
        return {'x': jax.random.normal(ks[0], (B, N, HIDDEN), jnp.float32), 'spatial_encoding': jax.random.normal(ks[1], (B, N, N), jnp.float32), 'edge_encoding': jax.random.normal(ks[2], (B, N, N), jnp.float32), 'Wq': jax.random.normal(ks[3], (HIDDEN, HIDDEN), jnp.float32) * s, 'Wk': jax.random.normal(ks[4], (HIDDEN, HIDDEN), jnp.float32) * s, 'Wv': jax.random.normal(ks[5], (HIDDEN, HIDDEN), jnp.float32) * s, 'bv': jax.random.normal(ks[6], (HIDDEN,), jnp.float32) * s, 'Wo': jax.random.normal(ks[7], (HIDDEN, HIDDEN), jnp.float32) * s, 'bo': jax.random.normal(ks[8], (HIDDEN,), jnp.float32) * s}
    _L0_gnn_all = _L0_gnn_setup()
    _L0_gnn_in = {k: v for k, v in _L0_gnn_all.items() if k in ('Wq', 'Wk', 'Wv', 'bv', 'Wo', 'bo')}
    del _L0_gnn_all

    def _L1_gnn_setup():
        import jax, jax.numpy as jnp
        import numpy as np
        B, L, H = (8, 1024, 384)
        LN_EPS = 1e-12
        key = jax.random.key(seed)
        ks = jax.random.split(key, 10)
        hidden_state = jax.random.normal(ks[0], (B, L, H), dtype=jnp.float32)
        adjacency = jax.random.randint(ks[1], (B, L, L), 0, 2).astype(jnp.float32)
        bound = 1.0 / np.sqrt(H)
        W_left = jax.random.normal(ks[2], (H, H), dtype=jnp.float32) * np.sqrt(2.0 / (H + H))
        b_left = jax.random.uniform(ks[3], (H,), minval=-bound, maxval=bound, dtype=jnp.float32)
        W_self = jax.random.normal(ks[4], (H, H), dtype=jnp.float32) * np.sqrt(2.0 / (H + H))
        b_self = jax.random.uniform(ks[5], (H,), minval=-bound, maxval=bound, dtype=jnp.float32)
        W_right = jax.random.normal(ks[6], (H, H), dtype=jnp.float32) * np.sqrt(2.0 / (H + H))
        b_right = jax.random.uniform(ks[7], (H,), minval=-bound, maxval=bound, dtype=jnp.float32)
        gamma = jnp.ones((H,), dtype=jnp.float32)
        beta = jnp.zeros((H,), dtype=jnp.float32)
        return {'hidden_state': hidden_state, 'adjacency': adjacency, 'W_left': W_left, 'b_left': b_left, 'W_self': W_self, 'b_self': b_self, 'W_right': W_right, 'b_right': b_right, 'gamma': gamma, 'beta': beta}
    _L1_gnn_all = _L1_gnn_setup()
    _L1_gnn_in = {k: v for k, v in _L1_gnn_all.items() if k in ('W_left', 'b_left', 'W_self', 'b_self', 'W_right', 'b_right', 'gamma', 'beta')}
    del _L1_gnn_all

    def _L2_gnn_setup():
        import jax, jax.numpy as jnp
        import numpy as np
        LN_EPS = 1e-12

        def _digcn_forward(hidden_state, adjacency_matrix, Wl, bl, Ws, bs, Wr, br, ln_w, ln_b):
            B, S, D = hidden_state.shape
            temper = jnp.asarray(D, jnp.float32) ** 0.5
            i = jnp.arange(S)
            upper = (i[None, :] > i[:, None]).astype(hidden_state.dtype)
            lower = (i[None, :] < i[:, None]).astype(hidden_state.dtype)

            def layer(h, params):
                wl, b_l, ws, b_s, wr, b_r, g, beta = params
                u = jnp.einsum('bid,bjd->bij', h, h) / temper
                a = jax.nn.softmax(u, axis=-1)
                delta = a * adjacency_matrix
                attn = delta / (jnp.sum(delta, axis=-1, keepdims=True) + 1e-10)
                hl = h @ wl.T + b_l
                hs = h @ ws.T + b_s
                hr = h @ wr.T + b_r
                diag_a = jnp.diagonal(attn, axis1=1, axis2=2)
                ctx = jnp.einsum('bij,bjd->bid', attn * upper, hl) + diag_a[..., None] * hs + jnp.einsum('bij,bjd->bid', attn * lower, hr)
                mean = ctx.mean(-1, keepdims=True)
                var = ctx.var(-1, keepdims=True)
                o = (ctx - mean) / jnp.sqrt(var + LN_EPS) * g + beta
                return (jax.nn.relu(o), None)
            out, _ = jax.lax.scan(layer, hidden_state, (Wl, bl, Ws, bs, Wr, br, ln_w, ln_b))
            return out
        key = jax.random.key(seed)
        ks = jax.random.split(key, 6)
        B, S, D, L = (8, 512, 384, 2)
        scale = (1.0 / D) ** 0.5
        hidden_state = jax.random.normal(ks[0], (B, S, D), jnp.float32)
        adjacency_matrix = (jax.random.uniform(ks[1], (B, S, S)) < 0.05).astype(jnp.float32)
        Wl = jax.random.normal(ks[2], (L, D, D), jnp.float32) * scale
        Ws = jax.random.normal(ks[3], (L, D, D), jnp.float32) * scale
        Wr = jax.random.normal(ks[4], (L, D, D), jnp.float32) * scale
        bl = jnp.zeros((L, D), jnp.float32)
        bs = jnp.zeros((L, D), jnp.float32)
        br = jnp.zeros((L, D), jnp.float32)
        ln_w = jnp.ones((L, D), jnp.float32)
        ln_b = jnp.zeros((L, D), jnp.float32)
        return dict(hidden_state=hidden_state, adjacency_matrix=adjacency_matrix, Wl=Wl, bl=bl, Ws=Ws, bs=bs, Wr=Wr, br=br, ln_w=ln_w, ln_b=ln_b)
    _L2_gnn_all = _L2_gnn_setup()
    _L2_gnn_in = {k: v for k, v in _L2_gnn_all.items() if k in ('Wl', 'bl', 'Ws', 'bs', 'Wr', 'br', 'ln_w', 'ln_b')}
    del _L2_gnn_all

    def _L3_gnn_setup():
        import jax, jax.numpy as jnp
        import numpy as np
        NUM_HEADS = 12
        HIDDEN = 384
        HEAD = HIDDEN // NUM_HEADS
        SCALE = HIDDEN ** (-0.5)
        key = jax.random.key(seed)
        ks = jax.random.split(key, 8)
        B, N = (16, 256)
        std = HIDDEN ** (-0.5)
        return {'x': jax.random.normal(ks[0], (B, N, HIDDEN), dtype=jnp.float32), 'encoding_bias': jax.random.normal(ks[1], (B, N, N), dtype=jnp.float32), 'Wq': jax.random.normal(ks[2], (HIDDEN, HIDDEN), dtype=jnp.float32) * std, 'Wk': jax.random.normal(ks[3], (HIDDEN, HIDDEN), dtype=jnp.float32) * std, 'Wv': jax.random.normal(ks[4], (HIDDEN, HIDDEN), dtype=jnp.float32) * std, 'bv': jax.random.normal(ks[5], (HIDDEN,), dtype=jnp.float32) * 0.01, 'Wo': jax.random.normal(ks[6], (HIDDEN, HIDDEN), dtype=jnp.float32) * std, 'bo': jax.random.normal(ks[7], (HIDDEN,), dtype=jnp.float32) * 0.01}
    _L3_gnn_all = _L3_gnn_setup()
    _L3_gnn_in = {k: v for k, v in _L3_gnn_all.items() if k in ('Wq', 'Wk', 'Wv', 'bv', 'Wo', 'bo')}
    del _L3_gnn_all
    return {'x': x, 'adj': adj, 'L0_gnn_Wq': _L0_gnn_in['Wq'], 'L0_gnn_Wk': _L0_gnn_in['Wk'], 'L0_gnn_Wv': _L0_gnn_in['Wv'], 'L0_gnn_bv': _L0_gnn_in['bv'], 'L0_gnn_Wo': _L0_gnn_in['Wo'], 'L0_gnn_bo': _L0_gnn_in['bo'], 'L1_gnn_W_left': _L1_gnn_in['W_left'], 'L1_gnn_b_left': _L1_gnn_in['b_left'], 'L1_gnn_W_self': _L1_gnn_in['W_self'], 'L1_gnn_b_self': _L1_gnn_in['b_self'], 'L1_gnn_W_right': _L1_gnn_in['W_right'], 'L1_gnn_b_right': _L1_gnn_in['b_right'], 'L1_gnn_gamma': _L1_gnn_in['gamma'], 'L1_gnn_beta': _L1_gnn_in['beta'], 'L2_gnn_Wl': _L2_gnn_in['Wl'], 'L2_gnn_bl': _L2_gnn_in['bl'], 'L2_gnn_Ws': _L2_gnn_in['Ws'], 'L2_gnn_bs': _L2_gnn_in['bs'], 'L2_gnn_Wr': _L2_gnn_in['Wr'], 'L2_gnn_br': _L2_gnn_in['br'], 'L2_gnn_ln_w': _L2_gnn_in['ln_w'], 'L2_gnn_ln_b': _L2_gnn_in['ln_b'], 'L3_gnn_Wq': _L3_gnn_in['Wq'], 'L3_gnn_Wk': _L3_gnn_in['Wk'], 'L3_gnn_Wv': _L3_gnn_in['Wv'], 'L3_gnn_bv': _L3_gnn_in['bv'], 'L3_gnn_Wo': _L3_gnn_in['Wo'], 'L3_gnn_bo': _L3_gnn_in['bo']}

def reference(x, adj, L0_gnn_Wq, L0_gnn_Wk, L0_gnn_Wv, L0_gnn_bv, L0_gnn_Wo, L0_gnn_bo, L1_gnn_W_left, L1_gnn_b_left, L1_gnn_W_self, L1_gnn_b_self, L1_gnn_W_right, L1_gnn_b_right, L1_gnn_gamma, L1_gnn_beta, L2_gnn_Wl, L2_gnn_bl, L2_gnn_Ws, L2_gnn_bs, L2_gnn_Wr, L2_gnn_br, L2_gnn_ln_w, L2_gnn_ln_b, L3_gnn_Wq, L3_gnn_Wk, L3_gnn_Wv, L3_gnn_bv, L3_gnn_Wo, L3_gnn_bo):
    import jax
    import jax.numpy as jnp

    def _L0_gnn_ref(x, spatial_encoding, edge_encoding, Wq, Wk, Wv, bv, Wo, bo):
        import jax, jax.numpy as jnp
        import numpy as np
        NUM_HEADS = 12
        HIDDEN = 384
        HEAD = HIDDEN // NUM_HEADS
        B, N = (16, 256)
        b, n, h = x.shape
        scale = jnp.asarray(HIDDEN, x.dtype) ** (-0.5)
        q = (x @ Wq.T).reshape(b, n, NUM_HEADS, HEAD)
        k = (x @ Wk.T).reshape(b, n, NUM_HEADS, HEAD)
        v = (x @ Wv.T + bv).reshape(b, n, NUM_HEADS, HEAD)
        bias = (spatial_encoding + edge_encoding)[:, None]
        scores = jnp.einsum('bqhd,bkhd->bhqk', q, k) * scale + bias
        row_nonzero = jnp.any(scores != 0, axis=-1, keepdims=True)
        scores = jnp.where(row_nonzero, scores, -jnp.inf)
        p = jax.nn.softmax(scores, axis=-1)
        p = jnp.nan_to_num(p)
        out = jnp.einsum('bhqk,bkhd->bqhd', p, v).reshape(b, n, h)
        return out @ Wo.T + bo

    def _L1_gnn_ref(hidden_state, adjacency, W_left, b_left, W_self, b_self, W_right, b_right, gamma, beta):
        import jax, jax.numpy as jnp
        import numpy as np
        B, L, H = (8, 1024, 384)
        LN_EPS = 1e-12
        h = hidden_state
        d = h.shape[-1]
        n = h.shape[1]
        u = jnp.einsum('bld,bmd->blm', h, h) / jnp.sqrt(jnp.asarray(d, h.dtype))
        p = jax.nn.softmax(u, axis=-1)
        delta = p * adjacency
        attn = delta / (jnp.sum(delta, axis=2, keepdims=True) + 1e-10)
        h_left = jnp.einsum('bld,ed->ble', h, W_left) + b_left
        h_self = jnp.einsum('bld,ed->ble', h, W_self) + b_self
        h_right = jnp.einsum('bld,ed->ble', h, W_right) + b_right
        i = jnp.arange(n)[:, None]
        j = jnp.arange(n)[None, :]
        attn_left = jnp.where(j > i, attn, 0.0)
        attn_right = jnp.where(j < i, attn, 0.0)
        diag_a = jnp.diagonal(attn, axis1=1, axis2=2)
        ctx = jnp.einsum('blm,bmd->bld', attn_left, h_left) + diag_a[..., None] * h_self + jnp.einsum('blm,bmd->bld', attn_right, h_right)
        mu = jnp.mean(ctx, axis=-1, keepdims=True)
        var = jnp.mean(jnp.square(ctx - mu), axis=-1, keepdims=True)
        o = (ctx - mu) / jnp.sqrt(var + LN_EPS) * gamma + beta
        return jax.nn.relu(o)

    def _L2_gnn_ref(hidden_state, adjacency_matrix, Wl, bl, Ws, bs, Wr, br, ln_w, ln_b):
        import jax, jax.numpy as jnp
        import numpy as np
        LN_EPS = 1e-12

        def _digcn_forward(hidden_state, adjacency_matrix, Wl, bl, Ws, bs, Wr, br, ln_w, ln_b):
            B, S, D = hidden_state.shape
            temper = jnp.asarray(D, jnp.float32) ** 0.5
            i = jnp.arange(S)
            upper = (i[None, :] > i[:, None]).astype(hidden_state.dtype)
            lower = (i[None, :] < i[:, None]).astype(hidden_state.dtype)

            def layer(h, params):
                wl, b_l, ws, b_s, wr, b_r, g, beta = params
                u = jnp.einsum('bid,bjd->bij', h, h) / temper
                a = jax.nn.softmax(u, axis=-1)
                delta = a * adjacency_matrix
                attn = delta / (jnp.sum(delta, axis=-1, keepdims=True) + 1e-10)
                hl = h @ wl.T + b_l
                hs = h @ ws.T + b_s
                hr = h @ wr.T + b_r
                diag_a = jnp.diagonal(attn, axis1=1, axis2=2)
                ctx = jnp.einsum('bij,bjd->bid', attn * upper, hl) + diag_a[..., None] * hs + jnp.einsum('bij,bjd->bid', attn * lower, hr)
                mean = ctx.mean(-1, keepdims=True)
                var = ctx.var(-1, keepdims=True)
                o = (ctx - mean) / jnp.sqrt(var + LN_EPS) * g + beta
                return (jax.nn.relu(o), None)
            out, _ = jax.lax.scan(layer, hidden_state, (Wl, bl, Ws, bs, Wr, br, ln_w, ln_b))
            return out
        return _digcn_forward(hidden_state, adjacency_matrix, Wl, bl, Ws, bs, Wr, br, ln_w, ln_b)

    def _L3_gnn_ref(x, encoding_bias, Wq, Wk, Wv, bv, Wo, bo):
        import jax, jax.numpy as jnp
        import numpy as np
        NUM_HEADS = 12
        HIDDEN = 384
        HEAD = HIDDEN // NUM_HEADS
        SCALE = HIDDEN ** (-0.5)
        B, N, _ = x.shape
        q = (x @ Wq.T).reshape(B, N, NUM_HEADS, HEAD)
        k = (x @ Wk.T).reshape(B, N, NUM_HEADS, HEAD)
        v = (x @ Wv.T + bv).reshape(B, N, NUM_HEADS, HEAD)
        a = jnp.einsum('bnhd,bmhd->bhnm', q, k) * SCALE + encoding_bias[:, None, :, :]
        pad_mask = jnp.all(a == 0, axis=-1)
        a = jnp.where(pad_mask[..., None], -jnp.inf, a)
        a = jax.nn.softmax(a, axis=-1)
        a = jnp.nan_to_num(a)
        o = jnp.einsum('bhnm,bmhd->bnhd', a, v).reshape(B, N, HIDDEN)
        return o @ Wo.T + bo
    h = jnp.maximum(_layernorm(x, axis=-1), 0.0)
    x = x + _L0_gnn_ref(h, adj, adj, L0_gnn_Wq, L0_gnn_Wk, L0_gnn_Wv, L0_gnn_bv, L0_gnn_Wo, L0_gnn_bo)
    h = jnp.maximum(_layernorm(x, axis=-1), 0.0)
    x = x + _L1_gnn_ref(h, adj, L1_gnn_W_left, L1_gnn_b_left, L1_gnn_W_self, L1_gnn_b_self, L1_gnn_W_right, L1_gnn_b_right, L1_gnn_gamma, L1_gnn_beta)
    h = jnp.maximum(_layernorm(x, axis=-1), 0.0)
    x = x + _L2_gnn_ref(h, adj, L2_gnn_Wl, L2_gnn_bl, L2_gnn_Ws, L2_gnn_bs, L2_gnn_Wr, L2_gnn_br, L2_gnn_ln_w, L2_gnn_ln_b)
    h = jnp.maximum(_layernorm(x, axis=-1), 0.0)
    x = x + _L3_gnn_ref(h, adj, L3_gnn_Wq, L3_gnn_Wk, L3_gnn_Wv, L3_gnn_bv, L3_gnn_Wo, L3_gnn_bo)
    return x

_drawn_inputs = setup_inputs


def setup_inputs(seed=0):
    import zlib

    import numpy as np

    out = dict(_drawn_inputs(seed))
    spreads = {'L1_gnn_gamma': (1.0, 0.2),
     'L1_gnn_beta': (0.0, 0.1),
     'L2_gnn_bl': (0.0, 0.735),
     'L2_gnn_bs': (0.0, 0.1),
     'L2_gnn_br': (0.0, 0.8),
     'L2_gnn_ln_w': (1.0, 0.2),
     'L2_gnn_ln_b': (0.0, 0.1)}
    factors = {'L0_gnn_Wq': 8.0,
     'L0_gnn_Wk': 8.0,
     'L0_gnn_bv': 6.953,
     'L0_gnn_bo': 2.961,
     'L1_gnn_W_left': 3.85,
     'L1_gnn_b_left': 58.179,
     'L1_gnn_W_right': 4.528,
     'L1_gnn_b_right': 64.0,
     'L3_gnn_Wq': 5.684,
     'L3_gnn_Wk': 5.693,
     'L3_gnn_bv': 8.0,
     'L3_gnn_bo': 8.0}
    for name, (base, spread) in spreads.items():
        noise = np.random.default_rng([zlib.crc32(name.encode()), seed]).standard_normal(out[name].shape)
        drawn = base * np.exp(spread * noise) if base else spread * noise
        out[name] = jnp.asarray(drawn.astype(out[name].dtype))
    for name, factor in factors.items():
        out[name] = (out[name] * factor).astype(out[name].dtype)
    return out
```

```python
from contextlib import ExitStack

import concourse.bass as bass
from concourse import mybir

F32 = mybir.dt.float32
ALU = mybir.AluOpType
ACT = mybir.ActivationFunctionType
AX = mybir.AxisListType

GRAPHS, NODES, FEATURES, HEADS = 64, 128, 384, 12
HEAD = FEATURES // HEADS
CHUNKS = FEATURES // 128
PER_CHUNK = HEADS // CHUNKS
GROUP = 4
GROUPS = GRAPHS // GROUP
WIDE = HEAD + 1
V_ROW = (HEADS - 1) * WIDE + 128
SCORES = HEADS
BANKS_PER_GROUP = GROUP * CHUNKS
SCALE = float(FEATURES) ** -0.5
EPS_IN, EPS_OUT, EPS_SUM = 1e-5, 1e-12, 1e-10
BIAS_TIMES = {"attention0": 2.0, "attention3": 1.0}
PASSES = ("attention0", "convolution1", "convolution2a", "convolution2b", "attention3")
WEIGHTS, VECTORS = 4, 5


def build(nc, x_in, adj_in, consts_in, weights_in, vectors_in, out):
    x1 = nc.dram_tensor("x_after_0", [GRAPHS, NODES, FEATURES], F32, kind="Internal").ap()
    x2 = nc.dram_tensor("x_after_1", [GRAPHS, NODES, FEATURES], F32, kind="Internal").ap()
    h2 = nc.dram_tensor("h_inside_2", [GRAPHS, NODES, FEATURES], F32, kind="Internal").ap()
    x3 = nc.dram_tensor("x_after_2", [GRAPHS, NODES, FEATURES], F32, kind="Internal").ap()
    source = (x_in, x1, x2, h2, x3)
    residual = (x_in, x1, None, x2, x3)
    target = (x1, x2, h2, x3, out)

    with ExitStack() as ctx:
        def sb(name, shape):
            return ctx.enter_context(nc.sbuf_tensor(name, shape, F32))

        def sem(name):
            return ctx.enter_context(nc.semaphore(name))

        consts = sb("consts", [128, 3, 128])
        ident = consts[:, 0, :]
        later = consts[:, 1, :]
        earlier = consts[:, 2, :]
        minus_half = sb("minus_half", [128, GROUP])
        weights = sb("weights", [128, 2, WEIGHTS, CHUNKS, FEATURES])
        vectors = sb("vectors", [128, 2, VECTORS, FEATURES])
        xs = sb("xs", [128, GROUP, FEATURES])
        res = sb("res", [128, GROUP, FEATURES])
        ys = sb("ys", [128, GROUP, FEATURES])
        hs = sb("hs", [128, GROUP, FEATURES])
        adj = sb("adj", [128, GROUP, NODES])
        stats = sb("stats", [128, GROUP, 6])
        moments = sb("moments", [128, GROUP, 2])
        var_eps = sb("var_eps", [128, GROUP])
        neg_mean = sb("neg_mean", [128, GROUP])
        rstd = sb("rstd", [128, GROUP])
        shift = sb("shift", [128, GROUP])
        spare = sb("spare", [128, 1])
        hT = sb("hT", [128, CHUNKS, GROUP, NODES])
        qT = sb("qT", [128, CHUNKS, GROUP, NODES])
        kT = sb("kT", [128, CHUNKS, GROUP, PER_CHUNK, NODES])
        values = sb("values", [128, GROUP, V_ROW])
        probs = sb("probs", [128, GROUP, HEADS, NODES])
        probsT = sb("probsT", [128, CHUNKS, PER_CHUNK, NODES])
        row_max = sb("row_max", [128, GROUP, HEADS])
        row_abs = sb("row_abs", [128, GROUP, HEADS])
        inv_sum = sb("inv_sum", [128, HEADS])
        inv_kept = sb("inv_kept", [128, HEADS])
        heads_out = sb("heads_out", [128, 2, FEATURES])
        heads_outT = sb("heads_outT", [128, 2, CHUNKS, NODES])
        gT = sb("gT", [128, 2, CHUNKS, NODES])
        left = sb("left", [128, FEATURES])
        right = sb("right", [128, FEATURES])
        own = sb("own", [128, FEATURES])
        e = sb("e", [128, NODES])
        e_adj = sb("e_adj", [128, NODES])
        attn = sb("attn", [128, NODES])
        attn_ident = sb("attn_ident", [128, NODES])
        attn_leftT = sb("attn_leftT", [128, NODES])
        attn_rightT = sb("attn_rightT", [128, NODES])
        neg_max = sb("neg_max", [128, 1])
        neg_max_scaled = sb("neg_max_scaled", [128, 1])
        e_sum = sb("e_sum", [128, 1])
        e_adj_sum = sb("e_adj_sum", [128, 1])
        denom = sb("denom", [128, 1])
        inv_denom = sb("inv_denom", [128, 1])
        diag = sb("diag", [128, 2])
        mixed = sb("mixed", [128, 2, FEATURES])
        normed = sb("normed", [128, FEATURES])
        o_stats = sb("o_stats", [128, 6])
        o_moments = sb("o_moments", [128, 2])
        o_var_eps = sb("o_var_eps", [128, 1])
        o_neg_mean = sb("o_neg_mean", [128, 1])
        o_rstd = sb("o_rstd", [128, 2])
        o_shift = sb("o_shift", [128, 2])

        bank = [ctx.enter_context(nc.psum_tensor(f"bank{i}", [128, 512], F32)) for i in range(8)]
        proj_bank, score_bank, probsT_bank = bank[0:2], bank[2:4], bank[4:6]
        heads_bank, tail_bank = bank[6], bank[7]
        left_bank, right_bank, own_bank, attnT_bank, gT_bank, u_bank, mix_bank = bank[0:7]

        consts_loaded = sem("consts_loaded")
        consts_set = sem("consts_set")
        params_loaded = [sem(f"params_loaded{p}") for p in range(len(PASSES))]
        pass_done = sem("pass_done")
        a_x_loaded, a_adj_loaded, a_y_stored = sem("a_x_loaded"), sem("a_adj_loaded"), sem("a_y_stored")
        a_bn, a_mv, a_var, a_rstd = sem("a_bn"), sem("a_mv"), sem("a_var"), sem("a_rstd")
        a_pow, a_h = sem("a_pow"), sem("a_h")
        hT_made, hT_kept, q_made, q_kept = sem("hT_made"), sem("hT_kept"), sem("q_made"), sem("q_kept")
        k_made, k_kept_act, k_kept_dve = sem("k_made"), sem("k_kept_act"), sem("k_kept_dve")
        v_made, v_kept = sem("v_made"), sem("v_kept")
        scores_made, scores_kept = sem("scores_made"), sem("scores_kept")
        max_found, abs_found, max_taken, exp_done = sem("max_found"), sem("abs_found"), sem("max_taken"), sem("exp_done")
        probsT_made, probsT_kept = sem("probsT_made"), sem("probsT_kept")
        heads_made, sums_inverted, sums_guarded, heads_kept = (
            sem("heads_made"), sem("sums_inverted"), sem("sums_guarded"), sem("heads_kept"))
        headsT_made, headsT_kept = sem("headsT_made"), sem("headsT_kept")
        y_made, a_y_kept, res_made = sem("y_made"), sem("a_y_kept"), sem("res_made")
        c_x_loaded, c_h_loaded = sem("c_x_loaded"), sem("c_h_loaded")
        c_adj_loaded = [sem(f"c_adj_loaded{b}") for b in range(GROUP)]
        c_res_loaded = [sem(f"c_res_loaded{b}") for b in range(GROUP)]
        c_y_stored = [sem(f"c_y_stored{b}") for b in range(GROUP)]
        c_bn, c_mv, c_var, c_rstd = sem("c_bn"), sem("c_mv"), sem("c_var"), sem("c_rstd")
        c_pow, c_h = sem("c_pow"), sem("c_h")
        gT_made, gT_kept, u_made = sem("gT_made"), sem("gT_kept"), sem("u_made")
        left_made, left_kept = sem("left_made"), sem("left_kept")
        right_made, right_kept = sem("right_made"), sem("right_kept")
        own_made, own_copied, own_kept = sem("own_made"), sem("own_copied"), sem("own_kept")
        u_max_found, u_max_scaled, u_exp_done = sem("u_max_found"), sem("u_max_scaled"), sem("u_exp_done")
        e_adj_done, denom_done, denom_inverted = sem("e_adj_done"), sem("denom_done"), sem("denom_inverted")
        attn_done, diag_done, attnT_made, attnT_kept = (
            sem("attn_done"), sem("diag_done"), sem("attnT_made"), sem("attnT_kept"))
        mix_made, mix_kept = sem("mix_made"), sem("mix_kept")
        o_bn, o_mv, o_var, o_pow, o_rstd_done = (
            sem("o_bn"), sem("o_mv"), sem("o_var"), sem("o_pow"), sem("o_rstd_done"))
        o_normed, o_scaled, o_shifted, c_y_kept = (
            sem("o_normed"), sem("o_scaled"), sem("o_shifted"), sem("c_y_kept"))

        def weight(p, w, c):
            return weights[:, p % 2, w, c, :]

        def vector(p, v):
            return vectors[:, p % 2, v, :]

        def finish_pass(eng, p):
            eng.drain().then_inc(pass_done, 1)
            eng.wait_ge(pass_done, 5 * (p + 1))

        def first_group(p):
            return GROUPS if PASSES[p] == "attention3" else 0 if p == 0 else GROUPS * (p - 1)

        def is_attention(p):
            return PASSES[p].startswith("attention")

        def normalises(p):
            return PASSES[p] != "convolution2b"

        def groups_of(eng, p, body):
            n0 = first_group(p)
            body(n0, 0, True, False)
            with eng.Fori(1, GROUPS - 1) as i:
                body(i + n0, i, False, False)
            body(n0 + GROUPS - 1, GROUPS - 1, False, True)

        block = ctx.enter_context(nc.Block())

        @block.sync
        def _(sp):
            def graphs(dram, i):
                return dram[bass.ts(i, GROUP)].rearrange("b n d -> n b d")

            def graph(dram, i, b):
                return dram[bass.ds(i * GROUP + b, 1)].rearrange("b n d -> (b n) d")

            def load_params(p):
                for w, m in enumerate(weights_in[p]):
                    sp.dma_start(weights[:, p % 2, w], m.rearrange("(c k) n -> k c n", k=128)
                                 ).then_inc(params_loaded[p], 16)
                for v, vec in enumerate(vectors_in[p]):
                    sp.dma_start(vector(p, v), vec.partition_broadcast(128)).then_inc(params_loaded[p], 16)

            def attention(p):
                n0 = first_group(p)
                sp.dma_start(xs[:], graphs(source[p], 0)).then_inc(a_x_loaded, 16)
                sp.dma_start(adj[:], graphs(adj_in, 0)).then_inc(a_adj_loaded, 16)
                if p == 0:
                    load_params(0)
                if p + 1 < len(PASSES):
                    load_params(p + 1)

                def body(n, i, first, last):
                    if not last:
                        sp.wait_ge(a_h, GROUP * n + GROUP)
                        sp.wait_ge(res_made, GROUP * n + GROUP)
                        sp.dma_start(xs[:], graphs(source[p], i + 1)).then_inc(a_x_loaded, 16)
                        sp.wait_ge(scores_kept, BANKS_PER_GROUP * n + BANKS_PER_GROUP)
                        sp.dma_start(adj[:], graphs(adj_in, i + 1)).then_inc(a_adj_loaded, 16)
                    sp.wait_ge(a_y_kept, GROUP * n + GROUP)
                    sp.dma_start(graphs(target[p], i), ys[:]).then_inc(a_y_stored, 16)

                groups_of(sp, p, body)
                sp.wait_ge(a_y_stored, 16 * (n0 + GROUPS))

            def convolution(p):
                n0 = first_group(p)
                r0 = n0 if p < 2 else n0 - GROUPS
                if normalises(p):
                    sp.dma_start(xs[:], graphs(source[p], 0)).then_inc(c_x_loaded, 16)
                else:
                    sp.dma_start(hs[:], graphs(source[p], 0)).then_inc(c_h_loaded, 16)
                for b in range(GROUP):
                    sp.dma_start(adj[:, b], graph(adj_in, 0, b)).then_inc(c_adj_loaded[b], 16)
                    if residual[p] is not None:
                        sp.dma_start(res[:, b], graph(residual[p], 0, b)).then_inc(c_res_loaded[b], 16)
                load_params(p + 1)

                def store(i, b, count, more):
                    sp.wait_ge(c_y_kept, count)
                    sp.dma_start(graph(target[p], i, b), ys[:, b]).then_inc(c_y_stored[b], 16)
                    if more and residual[p] is not None:
                        sp.dma_start(res[:, b], graph(residual[p], i + 1, b)).then_inc(c_res_loaded[b], 16)

                def body(n, i, first, last):
                    if not last and normalises(p):
                        sp.wait_ge(c_h, GROUP * n + GROUP)
                        sp.dma_start(xs[:], graphs(source[p], i + 1)).then_inc(c_x_loaded, 16)
                    for b in range(GROUP):
                        if not last:
                            sp.wait_ge(e_adj_done, GROUP * n + b + 1)
                            sp.dma_start(adj[:, b], graph(adj_in, i + 1, b)).then_inc(c_adj_loaded[b], 16)
                        if not last and not normalises(p) and b == GROUP - 1:
                            sp.wait_ge(gT_made, GROUP * n + GROUP)
                            sp.dma_start(hs[:], graphs(source[p], i + 1)).then_inc(c_h_loaded, 16)
                        if b > 0:
                            store(i, b - 1, GROUP * n + b, not last)
                        elif not first:
                            store(i - 1, GROUP - 1, GROUP * n, True)
                    if last:
                        store(i, GROUP - 1, GROUP * n + GROUP, False)

                groups_of(sp, p, body)
                for b in range(GROUP):
                    sp.wait_ge(c_y_stored[b], 16 * (n0 + GROUPS))

            sp.dma_start(consts[:], consts_in).then_inc(consts_loaded, 16)
            for p in range(len(PASSES)):
                (attention if is_attention(p) else convolution)(p)
                finish_pass(sp, p)

        @block.tensor
        def _(pe):
            def attention(p):
                WQ, WK, WV, WO = range(4)
                pe.wait_ge(params_loaded[p], 16 * (4 + 2))

                def transpose_h(n, first, chunks=range(CHUNKS)):
                    for c in chunks:
                        if c == 0:
                            pe.wait_ge(a_h, GROUP * n + GROUP)
                        if c < 2 and not first:
                            pe.wait_ge(v_kept, GROUP * n - GROUP + 3 + c)
                        if c == 2:
                            pe.wait_ge(hT_kept, CHUNKS * n + 1)
                        for b in range(GROUP):
                            mm = pe.transpose(proj_bank[c % 2][:, b * 128:(b + 1) * 128],
                                              hs[:, b, c * 128:(c + 1) * 128], ident)
                        mm.then_inc(hT_made, 1)

                def project_q(n):
                    for m in range(CHUNKS):
                        pe.wait_ge(hT_kept, CHUNKS * n + CHUNKS)
                        if m == 2:
                            pe.wait_ge(q_kept, CHUNKS * n + 1)
                        for c in range(CHUNKS):
                            mm = pe.matmul(proj_bank[(m + 1) % 2][:, :], weight(p, WQ, c)[:, m * 128:(m + 1) * 128],
                                           hT[:, c], start=c == 0, stop=c == CHUNKS - 1)
                        mm.then_inc(q_made, 1)

                def project_k(n, m):
                    if m < 2:
                        pe.wait_ge(q_kept, CHUNKS * n + m + 2)
                    else:
                        pe.wait_ge(k_kept_act, CHUNKS * n + 1)
                        pe.wait_ge(k_kept_dve, CHUNKS * n + 1)
                    for c in range(CHUNKS):
                        mm = pe.matmul(proj_bank[m % 2][:, :], weight(p, WK, c)[:, m * 128:(m + 1) * 128],
                                       hT[:, c], start=c == 0, stop=c == CHUNKS - 1)
                    mm.then_inc(k_made, 1)

                def project_v(n, b):
                    if b >= 2:
                        pe.wait_ge(v_kept, GROUP * n + b - 1)
                    for c in range(CHUNKS):
                        mm = pe.matmul(proj_bank[b % 2][:, 0:FEATURES], hT[:, c, b], weight(p, WV, c),
                                       start=c == 0, stop=c == CHUNKS - 1)
                    mm.then_inc(v_made, 1)

                def scores(n, b):
                    if b == 0:
                        pe.wait_ge(q_kept, CHUNKS * n + CHUNKS)
                        pe.wait_ge(k_kept_act, CHUNKS * n + CHUNKS)
                        pe.wait_ge(k_kept_dve, CHUNKS * n + CHUNKS)
                    for m in range(CHUNKS):
                        t = CHUNKS * b + m
                        pe.wait_ge(scores_kept, BANKS_PER_GROUP * n + max(t - 1, 0))
                        pe.matmul(score_bank[t % 2][:, :], qT[:, m, b], kT[:, m, b], start=True, stop=True
                                  ).then_inc(scores_made, 1)

                def transpose_probs(n, b, m):
                    t = CHUNKS * b + m
                    if m == 0:
                        pe.wait_ge(exp_done, GROUP * n + b + 1)
                    pe.wait_ge(probsT_kept, BANKS_PER_GROUP * n + max(t - 1, 0))
                    for g in range(PER_CHUNK):
                        mm = pe.transpose(probsT_bank[t % 2][:, g * 128:(g + 1) * 128],
                                          probs[:, b, m * PER_CHUNK + g], ident)
                    mm.then_inc(probsT_made, 1)

                def weigh_values(n, b, m):
                    if m == 0:
                        pe.wait_ge(v_kept, GROUP * n + b + 1)
                        pe.wait_ge(heads_kept, GROUP * n + b)
                    pe.wait_ge(probsT_kept, BANKS_PER_GROUP * n + CHUNKS * b + m + 1)
                    for g in range(PER_CHUNK):
                        at = (m * PER_CHUNK + g) * WIDE
                        mm = pe.matmul(heads_bank[:, at:at + 128], probsT[:, m, g], values[:, b, at:at + 128],
                                       start=True, stop=True)
                    if m == CHUNKS - 1:
                        mm.then_inc(heads_made, 1)

                def attend(n, b):
                    transpose_probs(n, b, 0)
                    transpose_probs(n, b, 1)
                    weigh_values(n, b, 0)
                    transpose_probs(n, b, 2)
                    weigh_values(n, b, 1)
                    weigh_values(n, b, 2)

                def project_out(n, b):
                    pe.wait_ge(heads_kept, GROUP * n + b + 1)
                    pe.wait_ge(a_y_kept, GROUP * n + b)
                    for c in range(CHUNKS):
                        mm = pe.transpose(tail_bank[:, c * 128:(c + 1) * 128],
                                          heads_out[:, b % 2, c * 128:(c + 1) * 128], ident)
                    mm.then_inc(headsT_made, 1)
                    pe.wait_ge(headsT_kept, GROUP * n + b + 1)
                    for c in range(CHUNKS):
                        mm = pe.matmul(tail_bank[:, 0:FEATURES], heads_outT[:, b % 2, c], weight(p, WO, c),
                                       start=c == 0, stop=c == CHUNKS - 1)
                    mm.then_inc(y_made, 1)

                def body(n, i, first, last):
                    scores(n, 0)
                    project_v(n, 0)
                    project_v(n, 1)
                    scores(n, 1)
                    project_v(n, 2)
                    project_v(n, 3)
                    scores(n, 2)
                    attend(n, 0)
                    scores(n, 3)
                    project_out(n, 0)
                    attend(n, 1)
                    if not last:
                        transpose_h(n + 1, False)
                    project_out(n, 1)
                    if not last:
                        project_q(n + 1)
                        project_k(n + 1, 0)
                    attend(n, 2)
                    if not last:
                        project_k(n + 1, 1)
                    project_out(n, 2)
                    attend(n, 3)
                    if not last:
                        project_k(n + 1, 2)
                    project_out(n, 3)

                n0 = first_group(p)
                transpose_h(n0, True)
                project_q(n0)
                for m in range(CHUNKS):
                    project_k(n0, m)
                groups_of(pe, p, body)

            def convolution(p):
                WL, WR, WS = range(3)
                pe.wait_ge(params_loaded[p], 16 * (3 + 5))

                def project(n, b, w, to, kept, made):
                    pe.wait_ge(kept, GROUP * n + b)
                    for c in range(CHUNKS):
                        mm = pe.matmul(to[:, 0:FEATURES], gT[:, b % 2, c], weight(p, w, c),
                                       start=c == 0, stop=c == CHUNKS - 1)
                    mm.then_inc(made, 1)

                def transpose_attn(n, b):
                    pe.wait_ge(attn_done, GROUP * n + b + 1)
                    pe.wait_ge(attnT_kept, GROUP * n + b)
                    pe.transpose(attnT_bank[:, 0:128], attn[:], ident).then_inc(attnT_made, 1)

                def transpose_g(n, b):
                    if normalises(p):
                        pe.wait_ge(c_h, GROUP * n + b + 1)
                    else:
                        pe.wait_ge(c_h_loaded, 16 * (n - first_group(p)) + 16)
                    pe.wait_ge(gT_kept, GROUP * n + b)
                    for c in range(CHUNKS):
                        mm = pe.transpose(gT_bank[:, c * 128:(c + 1) * 128], hs[:, b, c * 128:(c + 1) * 128], ident)
                    mm.then_inc(gT_made, 1)

                def gram(n, b):
                    pe.wait_ge(gT_kept, GROUP * n + b + 1)
                    pe.wait_ge(u_exp_done, GROUP * n + b)
                    for c in range(CHUNKS):
                        mm = pe.matmul(u_bank[:, 0:128], gT[:, b % 2, c], gT[:, b % 2, c],
                                       start=c == 0, stop=c == CHUNKS - 1)
                    mm.then_inc(u_made, 1)

                def mix(n, b):
                    pe.wait_ge(mix_kept, GROUP * n + b)
                    pe.wait_ge(attnT_kept, GROUP * n + b + 1)
                    pe.wait_ge(left_kept, GROUP * n + b + 1)
                    pe.matmul(mix_bank[:, 0:FEATURES], attn_leftT[:], left[:], start=True, stop=False)
                    pe.wait_ge(right_kept, GROUP * n + b + 1)
                    pe.matmul(mix_bank[:, 0:FEATURES], attn_rightT[:], right[:], start=False, stop=True
                              ).then_inc(mix_made, 1)

                def body(n, i, first, last):
                    for b in range(GROUP):
                        more = not (last and b == GROUP - 1)
                        n1, b1 = (n, b + 1) if b + 1 < GROUP else (n + 1, 0)
                        project(n, b, WL, left_bank, left_kept, left_made)
                        transpose_attn(n, b)
                        if more:
                            transpose_g(n1, b1)
                        project(n, b, WR, right_bank, right_kept, right_made)
                        project(n, b, WS, own_bank, own_copied, own_made)
                        if more:
                            gram(n1, b1)
                        mix(n, b)

                n0 = first_group(p)
                transpose_g(n0, 0)
                gram(n0, 0)
                groups_of(pe, p, body)

            pe.wait_ge(consts_loaded, 16)
            for p in range(len(PASSES)):
                (attention if is_attention(p) else convolution)(p)
                finish_pass(pe, p)

        @block.scalar
        def _(act):
            def normalise(n, b, ready, rstd_done):
                if b == 0:
                    act.wait_ge(rstd_done, n + 1)
                act.activation(hs[:, b], xs[:, b], ACT.Relu, bias=shift[:, b:b + 1],
                               scale=rstd[:, b:b + 1]).then_inc(ready, 1)

            def attention(p):
                def keep_hT(n):
                    for c in range(CHUNKS):
                        act.wait_ge(hT_made, CHUNKS * n + c + 1)
                        act.copy(hT[:, c].rearrange("p b n -> p (b n)"), proj_bank[c % 2][:, :]).then_inc(hT_kept, 1)

                def keep_q(n):
                    for m in range(CHUNKS):
                        act.wait_ge(q_made, CHUNKS * n + m + 1)
                        act.mul(qT[:, m].rearrange("p b n -> p (b n)"), proj_bank[(m + 1) % 2][:, :], SCALE
                                ).then_inc(q_kept, 1)

                def keep_k(n, m):
                    act.wait_ge(k_made, CHUNKS * n + m + 1)
                    for g in (0, 1):
                        ins = act.copy(kT[g * HEAD:(g + 1) * HEAD, m, :, g],
                                       proj_bank[m % 2][g * HEAD:(g + 1) * HEAD, :].rearrange("p (b n) -> p b n", b=GROUP))
                    ins.then_inc(k_kept_act, 1)

                def exponentials(n, b):
                    act.wait_ge(max_taken, GROUP * n + b + 1)
                    act.activation(probs[:, b], probs[:, b], ACT.Exp).then_inc(exp_done, 1)

                def keep_probsT(n, b):
                    for m in range(CHUNKS):
                        t = CHUNKS * b + m
                        act.wait_ge(probsT_made, BANKS_PER_GROUP * n + t + 1)
                        act.copy(probsT[:, m].rearrange("p g n -> p (g n)"), probsT_bank[t % 2][:, :]
                                 ).then_inc(probsT_kept, 1)

                def keep_headsT(n, b):
                    act.wait_ge(headsT_made, GROUP * n + b + 1)
                    act.copy(heads_outT[:, b % 2].rearrange("p c n -> p (c n)"), tail_bank[:, 0:FEATURES]
                             ).then_inc(headsT_kept, 1)

                def body(n, i, first, last):
                    exponentials(n, 0)
                    exponentials(n, 1)
                    keep_probsT(n, 0)
                    if not last:
                        for b in range(GROUP):
                            normalise(n + 1, b, a_h, a_rstd)
                    keep_headsT(n, 0)
                    exponentials(n, 2)
                    keep_probsT(n, 1)
                    if not last:
                        keep_hT(n + 1)
                    keep_headsT(n, 1)
                    exponentials(n, 3)
                    if not last:
                        keep_q(n + 1)
                        keep_k(n + 1, 0)
                    keep_probsT(n, 2)
                    if not last:
                        keep_k(n + 1, 1)
                    keep_headsT(n, 2)
                    keep_probsT(n, 3)
                    if not last:
                        keep_k(n + 1, 2)
                    keep_headsT(n, 3)

                n0 = first_group(p)
                for b in range(GROUP):
                    normalise(n0, b, a_h, a_rstd)
                keep_hT(n0)
                keep_q(n0)
                for m in range(CHUNKS):
                    keep_k(n0, m)
                groups_of(act, p, body)

            def convolution(p):
                def keep_gT(n, b):
                    act.wait_ge(gT_made, GROUP * n + b + 1)
                    act.copy(gT[:, b % 2].rearrange("p c n -> p (c n)"), gT_bank[:, 0:FEATURES]).then_inc(gT_kept, 1)

                def copy_own(n, b):
                    act.wait_ge(own_made, GROUP * n + b + 1)
                    act.wait_ge(mix_kept, GROUP * n + b)
                    act.copy(own[:], own_bank[:, 0:FEATURES]).then_inc(own_copied, 1)

                def exponentials(n, b):
                    act.wait_ge(u_max_found, GROUP * n + b + 1)
                    act.mul(neg_max_scaled[:], neg_max[:], SCALE).then_inc(u_max_scaled, 1)
                    act.wait_ge(u_max_scaled, GROUP * n + b + 1)
                    act.activation(e[:], u_bank[:, 0:128], ACT.Exp, bias=neg_max_scaled[:], scale=SCALE,
                                   accum_out=e_sum[:]).then_inc(u_exp_done, 1)

                def normalise_out(count, b):
                    act.wait_ge(o_rstd_done, count)
                    act.activation(normed[:], mixed[:, b % 2], ACT.Identity, bias=o_shift[:, b % 2:b % 2 + 1],
                                   scale=o_rstd[:, b % 2:b % 2 + 1]).then_inc(o_normed, 1)

                def body(n, i, first, last):
                    for b in range(GROUP):
                        more = not (last and b == GROUP - 1)
                        n1, b1 = (n, b + 1) if b + 1 < GROUP else (n + 1, 0)
                        if b > 0 or not first:
                            normalise_out(GROUP * n + b, (b - 1) % GROUP)
                        if more:
                            keep_gT(n1, b1)
                        copy_own(n, b)
                        if b == 2 and not last and normalises(p):
                            for b2 in range(GROUP):
                                normalise(n + 1, b2, c_h, c_rstd)
                        if more:
                            exponentials(n1, b1)
                    if last:
                        normalise_out(GROUP * n + GROUP, GROUP - 1)

                n0 = first_group(p)
                if normalises(p):
                    for b in range(GROUP):
                        normalise(n0, b, c_h, c_rstd)
                keep_gT(n0, 0)
                exponentials(n0, 0)
                groups_of(act, p, body)

            for p in range(len(PASSES)):
                (attention if is_attention(p) else convolution)(p)
                finish_pass(act, p)

        @block.gpsimd
        def _(pool):
            def reciprocal_deviation(n, var_done, pow_done, rstd_done):
                pool.wait_ge(var_done, n + 1)
                pool.tensor_tensor(rstd[:], var_eps[:], minus_half[:], ALU.pow).then_inc(pow_done, 1)
                pool.wait_ge(pow_done, n + 1)
                pool.tensor_tensor(shift[:], neg_mean[:], rstd[:], ALU.mult).then_inc(rstd_done, 1)

            def attention(p):
                BV, BO = range(2)
                pool.wait_ge(params_loaded[p], 16 * (4 + 2))

                def keep_residual(n):
                    pool.wait_ge(a_x_loaded, 16 * n + 16)
                    pool.wait_ge(a_y_kept, GROUP * n)
                    for b in range(GROUP):
                        pool.tensor_tensor(res[:, b], xs[:, b], vector(p, BO), ALU.add).then_inc(res_made, 1)

                def take_max(n, b):
                    pool.wait_ge(abs_found, GROUP * n + b + 1)
                    pool.tensor_tensor(probs[:, b], probs[:, b],
                                       row_max[:, b].unsqueeze(2).to_broadcast([128, HEADS, NODES]),
                                       ALU.subtract).then_inc(max_taken, 1)

                def body(n, i, first, last):
                    keep_residual(n)
                    take_max(n, 0)
                    take_max(n, 1)
                    if not last:
                        reciprocal_deviation(n + 1, a_var, a_pow, a_rstd)
                    take_max(n, 2)
                    take_max(n, 3)

                reciprocal_deviation(first_group(p), a_var, a_pow, a_rstd)
                groups_of(pool, p, body)

            def convolution(p):
                BL, BR, BS, GAMMA, BETA = range(5)
                pool.wait_ge(params_loaded[p], 16 * (3 + 5))

                def add_own_bias(n, b):
                    pool.wait_ge(own_copied, GROUP * n + b + 1)
                    pool.tensor_tensor(own[:], own[:], vector(p, BS), ALU.add).then_inc(own_kept, 1)

                def out_deviation(count, b):
                    pool.wait_ge(o_var, count)
                    pool.tensor_tensor(o_rstd[:, b % 2:b % 2 + 1], o_var_eps[:], minus_half[:, 0:1], ALU.pow
                                       ).then_inc(o_pow, 1)
                    pool.wait_ge(o_pow, count)
                    pool.tensor_tensor(o_shift[:, b % 2:b % 2 + 1], o_neg_mean[:], o_rstd[:, b % 2:b % 2 + 1],
                                       ALU.mult).then_inc(o_rstd_done, 1)

                def scale_and_shift(count):
                    pool.wait_ge(o_normed, count)
                    pool.tensor_tensor(normed[:], normed[:], vector(p, GAMMA), ALU.mult).then_inc(o_scaled, 1)
                    pool.wait_ge(o_scaled, count)
                    pool.tensor_tensor(normed[:], normed[:], vector(p, BETA), ALU.add).then_inc(o_shifted, 1)

                def body(n, i, first, last):
                    for b in range(GROUP):
                        if b > 0 or not first:
                            out_deviation(GROUP * n + b, (b - 1) % GROUP)
                            scale_and_shift(GROUP * n + b)
                        add_own_bias(n, b)
                        if b == 1 and not last and normalises(p):
                            reciprocal_deviation(n + 1, c_var, c_pow, c_rstd)
                    if last:
                        out_deviation(GROUP * n + GROUP, GROUP - 1)
                        scale_and_shift(GROUP * n + GROUP)

                if normalises(p):
                    reciprocal_deviation(first_group(p), c_var, c_pow, c_rstd)
                groups_of(pool, p, body)

            pool.memset(minus_half[:], -0.5)
            pool.memset(kT[:], 0.0)
            pool.memset(values[:], 0.0).then_inc(consts_set, 1)
            pool.wait_ge(consts_set, 1)
            pool.memset(values[:, :, 0:HEADS * WIDE].rearrange("p b (h w) -> p b h w", w=WIDE)[:, :, :, HEAD], 1.0
                        ).then_inc(consts_set, 1)
            for p in range(len(PASSES)):
                (attention if is_attention(p) else convolution)(p)
                finish_pass(pool, p)

        @block.vector
        def _(dve):
            def wait_in_memset(sem_, value):
                dve.wait_ge(sem_, value)
                dve.memset(spare[:], 0.0)

            def moments_of(n, loaded, bn, mv, var):
                dve.wait_ge(loaded, 16 * n + 16)
                for b in range(GROUP):
                    ins = dve.bn_stats(stats[:, b], xs[:, b])
                ins.then_inc(bn, 1)
                wait_in_memset(bn, n + 1)
                for b in range(GROUP):
                    ins = dve.bn_aggr(moments[:, b], stats[:, b])
                ins.then_inc(mv, 1)
                dve.wait_ge(mv, n + 1)
                dve.tensor_scalar(neg_mean[:], moments[:, :, 0], -1.0, None, ALU.mult)
                dve.tensor_scalar(var_eps[:], moments[:, :, 1], EPS_IN, None, ALU.add).then_inc(var, 1)

            def attention(p):
                BV, BO = range(2)
                dve.wait_ge(params_loaded[p], 16 * (4 + 2))
                n0 = first_group(p)

                def keep_k(n, m):
                    dve.wait_ge(k_made, CHUNKS * n + m + 1)
                    for g in (2, 3):
                        ins = dve.tensor_copy(kT[g * HEAD:(g + 1) * HEAD, m, :, g],
                                              proj_bank[m % 2][g * HEAD:(g + 1) * HEAD, :]
                                              .rearrange("p (b n) -> p b n", b=GROUP))
                    ins.then_inc(k_kept_dve, 1)

                def keep_v(n, b):
                    dve.wait_ge(v_made, GROUP * n + b + 1)
                    dve.tensor_tensor(values[:, b, 0:HEADS * WIDE].rearrange("p (h w) -> p h w", w=WIDE)[:, :, 0:HEAD],
                                      proj_bank[b % 2][:, 0:FEATURES].rearrange("p (h w) -> p h w", w=HEAD),
                                      vector(p, BV).rearrange("p (h w) -> p h w", w=HEAD), ALU.add).then_inc(v_kept, 1)

                def keep_scores(n, b):
                    if b == 0:
                        dve.wait_ge(a_adj_loaded, 16 * n + 16)
                    for m in range(CHUNKS):
                        t = CHUNKS * b + m
                        dve.wait_ge(scores_made, BANKS_PER_GROUP * n + t + 1)
                        dve.scalar_tensor_tensor(
                            out=probs[:, b, m * PER_CHUNK:(m + 1) * PER_CHUNK],
                            in0=adj[:, b].unsqueeze(1).to_broadcast([128, PER_CHUNK, NODES]),
                            scalar=BIAS_TIMES[PASSES[p]],
                            in1=score_bank[t % 2][:, :].rearrange("p (g n) -> p g n", g=PER_CHUNK),
                            op0=ALU.mult, op1=ALU.add).then_inc(scores_kept, 1)
                    dve.wait_ge(scores_kept, BANKS_PER_GROUP * n + CHUNKS * b + CHUNKS)
                    dve.tensor_reduce(row_max[:, b], probs[:, b], AX.X, ALU.max).then_inc(max_found, 1)
                    dve.tensor_reduce(row_abs[:, b], probs[:, b], AX.X, ALU.max, apply_absolute_value=True
                                      ).then_inc(abs_found, 1)

                def keep_heads(n, b):
                    sums = heads_bank[:, 0:HEADS * WIDE].rearrange("p (h w) -> p h w", w=WIDE)
                    dve.wait_ge(heads_made, GROUP * n + b + 1)
                    dve.reciprocal(inv_sum[:], sums[:, :, HEAD]).then_inc(sums_inverted, 1)
                    dve.wait_ge(sums_inverted, GROUP * n + b + 1)
                    dve.scalar_tensor_tensor(out=inv_kept[:], in0=row_abs[:, b], scalar=0.0, in1=inv_sum[:],
                                             op0=ALU.is_gt, op1=ALU.mult).then_inc(sums_guarded, 1)
                    dve.wait_ge(sums_guarded, GROUP * n + b + 1)
                    dve.tensor_tensor(heads_out[:, b % 2].rearrange("p (h w) -> p h w", w=HEAD), sums[:, :, 0:HEAD],
                                      inv_kept[:].unsqueeze(2).to_broadcast([128, HEADS, HEAD]), ALU.mult
                                      ).then_inc(heads_kept, 1)

                def keep_y(n, b):
                    if b == 0:
                        dve.wait_ge(a_y_stored, 16 * n)
                        dve.wait_ge(res_made, GROUP * n + GROUP)
                    dve.wait_ge(y_made, GROUP * n + b + 1)
                    dve.tensor_tensor(ys[:, b], tail_bank[:, 0:FEATURES], res[:, b], ALU.add).then_inc(a_y_kept, 1)

                def body(n, i, first, last):
                    keep_scores(n, 0)
                    keep_v(n, 0)
                    keep_v(n, 1)
                    keep_scores(n, 1)
                    keep_v(n, 2)
                    keep_v(n, 3)
                    if not last:
                        moments_of(n + 1, a_x_loaded, a_bn, a_mv, a_var)
                    keep_scores(n, 2)
                    keep_heads(n, 0)
                    keep_scores(n, 3)
                    keep_y(n, 0)
                    keep_heads(n, 1)
                    keep_y(n, 1)
                    if not last:
                        keep_k(n + 1, 0)
                    keep_heads(n, 2)
                    if not last:
                        keep_k(n + 1, 1)
                    keep_y(n, 2)
                    keep_heads(n, 3)
                    if not last:
                        keep_k(n + 1, 2)
                    keep_y(n, 3)

                moments_of(n0, a_x_loaded, a_bn, a_mv, a_var)
                for m in range(CHUNKS):
                    keep_k(n0, m)
                groups_of(dve, p, body)

            def convolution(p):
                BL, BR, BS, GAMMA, BETA = range(5)
                dve.wait_ge(params_loaded[p], 16 * (3 + 5))
                n0 = first_group(p)
                residuals = 0 if p == 1 else -GROUPS

                def keep_side(n, b, to, bank_, v, made, kept):
                    dve.wait_ge(made, GROUP * n + b + 1)
                    dve.tensor_tensor(to[:], bank_[:, 0:FEATURES], vector(p, v), ALU.add).then_inc(kept, 1)

                def split_attn(n, b):
                    dve.wait_ge(attnT_made, GROUP * n + b + 1)
                    dve.tensor_tensor(attn_leftT[:], attnT_bank[:, 0:128], later, ALU.mult)
                    dve.tensor_tensor(attn_rightT[:], attnT_bank[:, 0:128], earlier, ALU.mult).then_inc(attnT_kept, 1)

                def attention_rows(n, b):
                    dve.wait_ge(u_made, GROUP * n + b + 1)
                    dve.tensor_reduce(neg_max[:], u_bank[:, 0:128], AX.X, ALU.max, negate=True).then_inc(u_max_found, 1)
                    dve.wait_ge(c_adj_loaded[b], 16 * n + 16)
                    dve.wait_ge(u_exp_done, GROUP * n + b + 1)
                    dve.tensor_tensor_reduce(out=e_adj[:], in0=e[:], in1=adj[:, b], scale=1.0, scalar=0.0,
                                             op0=ALU.mult, op1=ALU.add, accum_out=e_adj_sum[:]).then_inc(e_adj_done, 1)
                    dve.wait_ge(e_adj_done, GROUP * n + b + 1)
                    dve.scalar_tensor_tensor(out=denom[:], in0=e_sum[:], scalar=EPS_SUM, in1=e_adj_sum[:],
                                             op0=ALU.mult, op1=ALU.add).then_inc(denom_done, 1)
                    dve.wait_ge(denom_done, GROUP * n + b + 1)
                    dve.reciprocal(inv_denom[:], denom[:]).then_inc(denom_inverted, 1)
                    dve.wait_ge(denom_inverted, GROUP * n + b + 1)
                    dve.tensor_scalar(attn[:], e_adj[:], inv_denom[:], None, ALU.mult).then_inc(attn_done, 1)
                    dve.wait_ge(attn_done, GROUP * n + b + 1)
                    dve.tensor_tensor_reduce(out=attn_ident[:], in0=attn[:], in1=ident, scale=1.0, scalar=0.0,
                                             op0=ALU.mult, op1=ALU.add, accum_out=diag[:, b % 2:b % 2 + 1]
                                             ).then_inc(diag_done, 1)

                def mix_own(n, b):
                    dve.wait_ge(own_kept, GROUP * n + b + 1)
                    dve.wait_ge(diag_done, GROUP * n + b + 1)
                    dve.wait_ge(mix_made, GROUP * n + b + 1)
                    dve.scalar_tensor_tensor(out=mixed[:, b % 2], in0=own[:], scalar=diag[:, b % 2:b % 2 + 1],
                                             in1=mix_bank[:, 0:FEATURES], op0=ALU.mult, op1=ALU.add
                                             ).then_inc(mix_kept, 1)
                    dve.wait_ge(mix_kept, GROUP * n + b + 1)
                    dve.bn_stats(o_stats[:], mixed[:, b % 2]).then_inc(o_bn, 1)
                    wait_in_memset(o_bn, GROUP * n + b + 1)
                    dve.bn_aggr(o_moments[:], o_stats[:]).then_inc(o_mv, 1)
                    dve.wait_ge(o_mv, GROUP * n + b + 1)
                    dve.tensor_scalar(o_neg_mean[:], o_moments[:, 0:1], -1.0, None, ALU.mult)
                    dve.tensor_scalar(o_var_eps[:], o_moments[:, 1:2], EPS_OUT, None, ALU.add).then_inc(o_var, 1)

                def keep_y(n, b, count):
                    dve.wait_ge(c_y_stored[b], 16 * n)
                    if residual[p] is not None:
                        dve.wait_ge(c_res_loaded[b], 16 * (n + residuals) + 16)
                    dve.wait_ge(o_shifted, count)
                    if residual[p] is not None:
                        dve.scalar_tensor_tensor(out=ys[:, b], in0=normed[:], scalar=0.0, in1=res[:, b],
                                                 op0=ALU.max, op1=ALU.add).then_inc(c_y_kept, 1)
                    else:
                        dve.tensor_scalar(ys[:, b], normed[:], 0.0, None, ALU.max).then_inc(c_y_kept, 1)

                def body(n, i, first, last):
                    for b in range(GROUP):
                        more = not (last and b == GROUP - 1)
                        n1, b1 = (n, b + 1) if b + 1 < GROUP else (n + 1, 0)
                        keep_side(n, b, left, left_bank, BL, left_made, left_kept)
                        split_attn(n, b)
                        keep_side(n, b, right, right_bank, BR, right_made, right_kept)
                        if b == 1 and not last and normalises(p):
                            moments_of(n + 1, c_x_loaded, c_bn, c_mv, c_var)
                        if more:
                            attention_rows(n1, b1)
                        if b > 0:
                            keep_y(n, b - 1, GROUP * n + b)
                        elif not first:
                            keep_y(n - 1, GROUP - 1, GROUP * n)
                        mix_own(n, b)
                    if last:
                        keep_y(n, GROUP - 1, GROUP * n + GROUP)

                if normalises(p):
                    moments_of(n0, c_x_loaded, c_bn, c_mv, c_var)
                attention_rows(n0, 0)
                groups_of(dve, p, body)

            dve.wait_ge(consts_set, 2)
            dve.wait_ge(consts_loaded, 16)
            for p in range(len(PASSES)):
                (attention if is_attention(p) else convolution)(p)
                finish_pass(dve, p)


def kernel(x, adj, L0_gnn_Wq, L0_gnn_Wk, L0_gnn_Wv, L0_gnn_bv, L0_gnn_Wo, L0_gnn_bo, L1_gnn_W_left, L1_gnn_b_left,
           L1_gnn_W_self, L1_gnn_b_self, L1_gnn_W_right, L1_gnn_b_right, L1_gnn_gamma, L1_gnn_beta, L2_gnn_Wl,
           L2_gnn_bl, L2_gnn_Ws, L2_gnn_bs, L2_gnn_Wr, L2_gnn_br, L2_gnn_ln_w, L2_gnn_ln_b, L3_gnn_Wq, L3_gnn_Wk,
           L3_gnn_Wv, L3_gnn_bv, L3_gnn_Wo, L3_gnn_bo):
    import numpy as np
    import concourse.bacc as bacc
    from concourse.bass_utils import run_bass_kernel_spmd

    nc = bacc.Bacc("TRN2", target_bir_lowering=False, num_devices=1)
    arrays = {}

    def give(name, a):
        arrays[name] = np.ascontiguousarray(a)
        return nc.dram_tensor(name, arrays[name].shape, mybir.dt.from_np(arrays[name].dtype),
                              kind="ExternalInput").ap()

    row, column = np.indices((128, 128))
    consts = np.stack([row == column, row > column, row < column], axis=1).astype(np.float32)
    weights = (
        (L0_gnn_Wq, L0_gnn_Wk, L0_gnn_Wv, L0_gnn_Wo),
        (L1_gnn_W_left, L1_gnn_W_right, L1_gnn_W_self),
        (L2_gnn_Wl[0], L2_gnn_Wr[0], L2_gnn_Ws[0]),
        (L2_gnn_Wl[1], L2_gnn_Wr[1], L2_gnn_Ws[1]),
        (L3_gnn_Wq, L3_gnn_Wk, L3_gnn_Wv, L3_gnn_Wo),
    )
    vectors = (
        (L0_gnn_bv, L0_gnn_bo),
        (L1_gnn_b_left, L1_gnn_b_right, L1_gnn_b_self, L1_gnn_gamma, L1_gnn_beta),
        (L2_gnn_bl[0], L2_gnn_br[0], L2_gnn_bs[0], L2_gnn_ln_w[0], L2_gnn_ln_b[0]),
        (L2_gnn_bl[1], L2_gnn_br[1], L2_gnn_bs[1], L2_gnn_ln_w[1], L2_gnn_ln_b[1]),
        (L3_gnn_bv, L3_gnn_bo),
    )
    weight_aps = [[give(f"weight{p}_{w}", np.asarray(m).T) for w, m in enumerate(ms)] for p, ms in enumerate(weights)]
    vector_aps = [[give(f"vector{p}_{v}", np.asarray(m)) for v, m in enumerate(vs)] for p, vs in enumerate(vectors)]
    x_ap, adj_ap, consts_ap = give("x_in", x), give("adj_in", adj), give("consts_in", consts)
    out = nc.dram_tensor("y_out", (GRAPHS, NODES, FEATURES), F32, kind="ExternalOutput").ap()
    build(nc, x_ap, adj_ap, consts_ap, weight_aps, vector_aps, out)
    return run_bass_kernel_spmd(nc, [arrays], core_ids=[0]).results[0]["y_out"]
```

```python
from contextlib import ExitStack

import concourse.bass as bass
from concourse import mybir

F32 = mybir.dt.float32
F32R = mybir.dt.float32r
ALU = mybir.AluOpType
ACT = mybir.ActivationFunctionType
AX = mybir.AxisListType

GRAPHS, NODES, FEATURES, HEADS = 64, 128, 384, 12
HEAD = FEATURES // HEADS
CHUNKS = FEATURES // 128
PER_CHUNK = HEADS // CHUNKS
GROUP = 4
GROUPS = GRAPHS // GROUP
SCORES = HEADS
BANKS_PER_GROUP = GROUP * CHUNKS
SCALE = float(FEATURES) ** -0.5
EPS_IN, EPS_OUT, EPS_SUM = 1e-5, 1e-12, 1e-10
BIAS_TIMES = {"attention0": 2.0, "attention3": 1.0}
PASSES = ("attention0", "convolution1", "convolution2a", "convolution2b", "attention3")
WEIGHTS, VECTORS = 4, 5


def build(nc, x_in, adj_in, consts_in, weights_in, vectors_in, out):
    x1 = nc.dram_tensor("x_after_0", [GRAPHS, NODES, FEATURES], F32, kind="Internal").ap()
    x2 = nc.dram_tensor("x_after_1", [GRAPHS, NODES, FEATURES], F32, kind="Internal").ap()
    h2 = nc.dram_tensor("h_inside_2", [GRAPHS, NODES, FEATURES], F32, kind="Internal").ap()
    x3 = nc.dram_tensor("x_after_2", [GRAPHS, NODES, FEATURES], F32, kind="Internal").ap()
    source = (x_in, x1, x2, h2, x3)
    residual = (x_in, x1, None, x2, x3)
    target = (x1, x2, h2, x3, out)

    with ExitStack() as ctx:
        def sb(name, shape, dtype=F32):
            return ctx.enter_context(nc.sbuf_tensor(name, shape, dtype))

        def sem(name):
            return ctx.enter_context(nc.semaphore(name))

        consts = sb("consts", [128, 3, 128])
        ident = consts[:, 0, :]
        later = consts[:, 1, :]
        earlier = consts[:, 2, :]
        minus_half = sb("minus_half", [128, GROUP])
        weights = sb("weights", [128, WEIGHTS, CHUNKS, FEATURES])
        weights_high = sb("weights_high", [128, WEIGHTS, CHUNKS, FEATURES], F32R)
        weights_low = sb("weights_low", [128, WEIGHTS, CHUNKS, FEATURES], F32R)
        vectors = sb("vectors", [128, 2, VECTORS, FEATURES])
        xs = sb("xs", [128, GROUP, FEATURES])
        held_x = sb("held_x", [128, GROUP // 2, FEATURES])
        res = sb("res", [128, GROUP, FEATURES])
        ys = sb("ys", [128, GROUP, FEATURES])
        hs = sb("hs", [128, GROUP, FEATURES])
        adj = sb("adj", [128, GROUP, NODES])
        stats = sb("stats", [128, GROUP, 6])
        moments = sb("moments", [128, GROUP, 2])
        var_eps = sb("var_eps", [128, GROUP])
        neg_mean = sb("neg_mean", [128, GROUP])
        rstd = sb("rstd", [128, GROUP])
        shift = sb("shift", [128, GROUP])
        spare = sb("spare", [128, 1])
        hT_high = sb("hT_high", [128, CHUNKS, GROUP, NODES], F32R)
        hT_low = sb("hT_low", [128, CHUNKS, GROUP, NODES], F32R)
        qT = sb("qT", [128, CHUNKS, GROUP, NODES])
        kT = sb("kT", [128, CHUNKS, GROUP, PER_CHUNK, NODES])
        values = sb("values", [128, GROUP, HEADS, 128])
        probs = sb("probs", [128, GROUP, HEADS, NODES])
        probsT = sb("probsT", [128, CHUNKS, PER_CHUNK, NODES])
        row_max = sb("row_max", [128, GROUP, HEADS])
        row_abs = sb("row_abs", [128, GROUP, HEADS])
        row_sum = sb("row_sum", [128, GROUP, HEADS])
        inv_sum = sb("inv_sum", [128, GROUP, HEADS])
        inv_kept = sb("inv_kept", [128, GROUP, HEADS])
        headsT_high = sb("headsT_high", [128, 2, CHUNKS, NODES], F32R)
        headsT_low = sb("headsT_low", [128, 2, CHUNKS, NODES], F32R)
        scratch = probs[:].rearrange("p b h n -> p (b h n)")
        left, right, own, normed = (scratch[:, k * FEATURES:(k + 1) * FEATURES] for k in range(4))
        mixed = scratch[:, 4 * FEATURES:6 * FEATURES].rearrange("p (b d) -> p b d", b=2)
        gT = scratch[:, 6 * FEATURES:8 * FEATURES].rearrange("p (b c n) -> p b c n", b=2, c=CHUNKS)
        e, e_adj, attn, attn_ident, attn_leftT, attn_rightT = (
            scratch[:, 8 * FEATURES + k * NODES:8 * FEATURES + (k + 1) * NODES] for k in range(6))
        gT_high = hT_high[:].rearrange("p c b n -> p (c b) n")[:, 0:2 * CHUNKS].rearrange("p (b c) n -> p b c n", b=2)
        gT_low = hT_low[:].rearrange("p c b n -> p (c b) n")[:, 0:2 * CHUNKS].rearrange("p (b c) n -> p b c n", b=2)
        neg_max = sb("neg_max", [128, 1])
        neg_max_scaled = sb("neg_max_scaled", [128, 1])
        e_sum = sb("e_sum", [128, 1])
        e_adj_sum = sb("e_adj_sum", [128, 1])
        denom = sb("denom", [128, 1])
        inv_denom = sb("inv_denom", [128, 1])
        diag = sb("diag", [128, 2])
        o_stats = sb("o_stats", [128, 6])
        o_moments = sb("o_moments", [128, 2])
        o_var_eps = sb("o_var_eps", [128, 1])
        o_neg_mean = sb("o_neg_mean", [128, 1])
        o_rstd = sb("o_rstd", [128, 2])
        o_shift = sb("o_shift", [128, 2])

        bank = [ctx.enter_context(nc.psum_tensor(f"bank{i}", [128, 512], F32)) for i in range(8)]
        proj_bank, score_bank, probsT_bank = bank[0:2], bank[2:4], bank[4:6]
        headsT_bank, y_bank = bank[6], bank[7]
        left_bank, right_bank, own_bank, attnT_bank, gT_bank, u_bank, mix_bank = bank[0:7]

        consts_loaded = sem("consts_loaded")
        consts_set = sem("consts_set")
        params_loaded = [sem(f"params_loaded{p}") for p in range(len(PASSES))]
        pass_done = sem("pass_done")
        weights_rounded, weights_split = sem("weights_rounded"), sem("weights_split")
        a_x_loaded, a_adj_loaded, x_held = sem("a_x_loaded"), sem("a_adj_loaded"), sem("x_held")
        a_y_stored = [sem(f"a_y_stored{half}") for half in range(2)]
        a_bn, a_mv, a_var, a_rstd = sem("a_bn"), sem("a_mv"), sem("a_var"), sem("a_rstd")
        a_pow, a_h = sem("a_pow"), sem("a_h")
        hT_made, hT_rounded, hT_kept = sem("hT_made"), sem("hT_rounded"), sem("hT_kept")
        q_made, q_kept = sem("q_made"), sem("q_kept")
        k_made, k_kept_act, k_kept_dve = sem("k_made"), sem("k_kept_act"), sem("k_kept_dve")
        v_made, v_kept = sem("v_made"), sem("v_kept")
        scores_made, scores_kept = sem("scores_made"), sem("scores_kept")
        max_found, abs_found, max_taken, exp_done = sem("max_found"), sem("abs_found"), sem("max_taken"), sem("exp_done")
        sums_found, sums_inverted, sums_guarded, probs_ready = sem("sums_found"), sem("sums_inverted"), sem("sums_guarded"), sem("probs_ready")
        probsT_made, probsT_kept = sem("probsT_made"), sem("probsT_kept")
        headsT_made, headsT_rounded, headsT_kept = sem("headsT_made"), sem("headsT_rounded"), sem("headsT_kept")
        y_made, a_y_kept, res_made = sem("y_made"), sem("a_y_kept"), sem("res_made")
        c_x_loaded = sem("c_x_loaded")
        c_h_loaded = [sem(f"c_h_loaded{b}") for b in range(GROUP)]
        c_adj_loaded = [sem(f"c_adj_loaded{b}") for b in range(GROUP)]
        c_res_loaded = [sem(f"c_res_loaded{b}") for b in range(GROUP)]
        c_y_stored = [sem(f"c_y_stored{b}") for b in range(GROUP)]
        c_bn, c_mv, c_var, c_rstd = sem("c_bn"), sem("c_mv"), sem("c_var"), sem("c_rstd")
        c_pow, c_h = sem("c_pow"), sem("c_h")
        gT_made, gT_kept, gT_rounded = sem("gT_made"), sem("gT_kept"), sem("gT_rounded")
        gT_split, u_made = sem("gT_split"), sem("u_made")
        left_made, left_kept = sem("left_made"), sem("left_kept")
        right_made, right_kept = sem("right_made"), sem("right_kept")
        own_made, own_copied, own_kept = sem("own_made"), sem("own_copied"), sem("own_kept")
        u_max_found, u_max_scaled, u_exp_done = sem("u_max_found"), sem("u_max_scaled"), sem("u_exp_done")
        e_adj_done, denom_done, denom_inverted = sem("e_adj_done"), sem("denom_done"), sem("denom_inverted")
        attn_done, diag_done, attnT_made, attnT_kept = (
            sem("attn_done"), sem("diag_done"), sem("attnT_made"), sem("attnT_kept"))
        mix_made, mix_kept = sem("mix_made"), sem("mix_kept")
        o_bn, o_mv, o_var, o_pow, o_rstd_done = (
            sem("o_bn"), sem("o_mv"), sem("o_var"), sem("o_pow"), sem("o_rstd_done"))
        o_normed, o_scaled, o_shifted, c_y_kept = (
            sem("o_normed"), sem("o_scaled"), sem("o_shifted"), sem("c_y_kept"))

        matrices = [len(ms) for ms in weights_in]

        def params(p):
            return 16 * (len(weights_in[p]) + len(vectors_in[p]))

        def flat(ap):
            return ap.rearrange("p a b -> p (a b)")

        def vector(p, v):
            return vectors[:, p % 2, v, :]

        def finish_pass(eng, p):
            eng.drain().then_inc(pass_done, 1)
            eng.wait_ge(pass_done, 5 * (p + 1))

        def first_group(p):
            return GROUPS if PASSES[p] == "attention3" else 0 if p == 0 else GROUPS * (p - 1)

        def is_attention(p):
            return PASSES[p].startswith("attention")

        def normalises(p):
            return PASSES[p] != "convolution2b"

        def groups_of(eng, p, body):
            n0 = first_group(p)
            body(n0, 0, True, False)
            with eng.Fori(1, GROUPS - 1) as i:
                body(i + n0, i, False, False)
            body(n0 + GROUPS - 1, GROUPS - 1, False, True)

        block = ctx.enter_context(nc.Block())

        @block.sync
        def _(sp):
            def graphs(dram, i):
                return dram[bass.ts(i, GROUP)].rearrange("b n d -> n b d")

            def graph(dram, i, b):
                return dram[bass.ds(i * GROUP + b, 1)].rearrange("b n d -> (b n) d")

            def load_params(p):
                for w, m in enumerate(weights_in[p]):
                    sp.dma_start(weights[:, w], m.rearrange("(c k) n -> k c n", k=128)
                                 ).then_inc(params_loaded[p], 16)
                for v, vec in enumerate(vectors_in[p]):
                    sp.dma_start(vector(p, v), vec.partition_broadcast(128)).then_inc(params_loaded[p], 16)

            def attention(p):
                n0 = first_group(p)
                sp.dma_start(xs[:], graphs(source[p], 0)).then_inc(a_x_loaded, 16)
                sp.dma_start(adj[:], graphs(adj_in, 0)).then_inc(a_adj_loaded, 16)
                if p == 0:
                    load_params(0)
                if p + 1 < len(PASSES):
                    sp.wait_ge(weights_split, sum(matrices[:p + 1]))
                    load_params(p + 1)

                pairs = target[p].rearrange("(i h b) n d -> h n i b d", h=2, b=2)

                def store(n, i, half):
                    sp.wait_ge(a_y_kept, GROUP * n + 2 * half + 2)
                    sp.dma_start(pairs[half, :, i], ys[:, 2 * half:2 * half + 2]).then_inc(a_y_stored[half], 16)

                def body(n, i, first, last):
                    if not last:
                        sp.wait_ge(x_held, 2 * n + 2)
                        sp.dma_start(xs[:], graphs(source[p], i + 1)).then_inc(a_x_loaded, 16)
                    if not first:
                        store(n - 1, i - 1, 1)
                    if not last:
                        sp.wait_ge(scores_kept, BANKS_PER_GROUP * n + BANKS_PER_GROUP)
                        sp.dma_start(adj[:], graphs(adj_in, i + 1)).then_inc(a_adj_loaded, 16)
                    store(n, i, 0)
                    if last:
                        store(n, i, 1)

                groups_of(sp, p, body)
                for half in range(2):
                    sp.wait_ge(a_y_stored[half], 16 * (n0 + GROUPS))

            def convolution(p):
                n0 = first_group(p)
                if normalises(p):
                    sp.dma_start(xs[:], graphs(source[p], 0)).then_inc(c_x_loaded, 16)
                for b in range(GROUP):
                    if not normalises(p):
                        sp.dma_start(hs[:, b], graph(source[p], 0, b)).then_inc(c_h_loaded[b], 16)
                    sp.dma_start(adj[:, b], graph(adj_in, 0, b)).then_inc(c_adj_loaded[b], 16)
                    if residual[p] is not None:
                        sp.dma_start(res[:, b], graph(residual[p], 0, b)).then_inc(c_res_loaded[b], 16)
                sp.wait_ge(weights_split, sum(matrices[:p + 1]))
                load_params(p + 1)

                def store(i, b, count, more):
                    sp.wait_ge(c_y_kept, count)
                    sp.dma_start(graph(target[p], i, b), ys[:, b]).then_inc(c_y_stored[b], 16)
                    if more and residual[p] is not None:
                        sp.dma_start(res[:, b], graph(residual[p], i + 1, b)).then_inc(c_res_loaded[b], 16)

                def body(n, i, first, last):
                    if not last and normalises(p):
                        sp.wait_ge(c_h, GROUP * n + GROUP)
                        sp.dma_start(xs[:], graphs(source[p], i + 1)).then_inc(c_x_loaded, 16)
                    for b in range(GROUP):
                        if not last:
                            sp.wait_ge(e_adj_done, GROUP * n + b + 1)
                            sp.dma_start(adj[:, b], graph(adj_in, i + 1, b)).then_inc(c_adj_loaded[b], 16)
                        if not last and not normalises(p):
                            sp.wait_ge(gT_made, GROUP * n + b + 1)
                            sp.dma_start(hs[:, b], graph(source[p], i + 1, b)).then_inc(c_h_loaded[b], 16)
                        if b > 0:
                            store(i, b - 1, GROUP * n + b, not last)
                        elif not first:
                            store(i - 1, GROUP - 1, GROUP * n, True)
                    if last:
                        store(i, GROUP - 1, GROUP * n + GROUP, False)

                groups_of(sp, p, body)
                for b in range(GROUP):
                    sp.wait_ge(c_y_stored[b], 16 * (n0 + GROUPS))

            sp.dma_start(consts[:], consts_in).then_inc(consts_loaded, 16)
            for p in range(len(PASSES)):
                (attention if is_attention(p) else convolution)(p)
                finish_pass(sp, p)

        @block.tensor
        def _(pe):
            def product(to, left_high, left_low, right_high, right_low, c):
                pe.matmul(to, left_high, right_high, start=c == 0, stop=False)
                pe.matmul(to, left_high, right_low, start=False, stop=False)
                return pe.matmul(to, left_low, right_high, start=False, stop=c == CHUNKS - 1)

            def attention(p):
                WQ, WK, WV, WO = range(4)
                pe.wait_ge(weights_split, sum(matrices[:p + 1]))

                def transpose_h(n, c, first):
                    if c == 0:
                        pe.wait_ge(a_h, GROUP * n + GROUP)
                    if c < 2 and not first:
                        pe.wait_ge(v_kept, GROUP * n - GROUP + 3 + c)
                    if c == 2:
                        pe.wait_ge(hT_kept, CHUNKS * n + 1)
                    for b in range(GROUP):
                        mm = pe.transpose(proj_bank[c % 2][:, b * 128:(b + 1) * 128],
                                          hs[:, b, c * 128:(c + 1) * 128], ident)
                    mm.then_inc(hT_made, 1)

                def project_chunk(n, w, m, to, made):
                    at = slice(m * 128, (m + 1) * 128)
                    for c in range(CHUNKS):
                        if w == WQ and m == 0:
                            pe.wait_ge(hT_kept, CHUNKS * n + c + 1)
                        mm = product(to[:, :], weights_high[:, w, c, at], weights_low[:, w, c, at],
                                     hT_high[:, c], hT_low[:, c], c)
                    mm.then_inc(made, 1)

                def project_q(n, m):
                    if m == 0:
                        pe.wait_ge(hT_kept, CHUNKS * n + 2)
                    elif m == 2:
                        pe.wait_ge(q_kept, CHUNKS * n + 1)
                    project_chunk(n, WQ, m, proj_bank[(m + 1) % 2], q_made)

                def project_k(n, m):
                    if m < 2:
                        pe.wait_ge(q_kept, CHUNKS * n + m + 2)
                    else:
                        pe.wait_ge(k_kept_act, CHUNKS * n + 1)
                        pe.wait_ge(k_kept_dve, CHUNKS * n + 1)
                    project_chunk(n, WK, m, proj_bank[m % 2], k_made)

                def project_v(n, b):
                    if b >= 2:
                        pe.wait_ge(v_kept, GROUP * n + b - 1)
                    for c in range(CHUNKS):
                        mm = product(proj_bank[b % 2][:, 0:FEATURES], hT_high[:, c, b], hT_low[:, c, b],
                                     weights_high[:, WV, c], weights_low[:, WV, c], c)
                    mm.then_inc(v_made, 1)

                def scores(n, b, m):
                    if b == 0:
                        pe.wait_ge(q_kept, CHUNKS * n + m + 1)
                        pe.wait_ge(k_kept_act, CHUNKS * n + m + 1)
                        pe.wait_ge(k_kept_dve, CHUNKS * n + m + 1)
                    t = CHUNKS * b + m
                    pe.wait_ge(scores_kept, BANKS_PER_GROUP * n + max(t - 1, 0))
                    pe.matmul(score_bank[t % 2][:, :], qT[:, m, b], kT[:, m, b], start=True, stop=True
                              ).then_inc(scores_made, 1)

                def transpose_probs(n, b, m):
                    t = CHUNKS * b + m
                    if m == 0:
                        pe.wait_ge(probs_ready, GROUP * n + b + 1)
                    pe.wait_ge(probsT_kept, BANKS_PER_GROUP * n + max(t - 1, 0))
                    for g in range(PER_CHUNK):
                        mm = pe.transpose(probsT_bank[t % 2][:, g * 128:(g + 1) * 128],
                                          probs[:, b, m * PER_CHUNK + g], ident)
                    mm.then_inc(probsT_made, 1)

                def weigh_values(n, b, m):
                    if m == 0:
                        pe.wait_ge(v_kept, GROUP * n + b + 1)
                        pe.wait_ge(headsT_kept, GROUP * n + b)
                    pe.wait_ge(probsT_kept, BANKS_PER_GROUP * n + CHUNKS * b + m + 1)
                    row = values[:, b].rearrange("p h w -> p (h w)")
                    for g in range(PER_CHUNK):
                        at = (m * PER_CHUNK + g) * 128 - g * HEAD
                        mm = pe.matmul(headsT_bank[:, m * 128:(m + 1) * 128], row[:, at:at + 128], probsT[:, m, g],
                                       start=g == 0, stop=g == PER_CHUNK - 1)
                    if m == CHUNKS - 1:
                        mm.then_inc(headsT_made, 1)

                def attend_and_project(n, b, between=None):
                    transpose_probs(n, b, 0)
                    transpose_probs(n, b, 1)
                    if between:
                        between()
                    weigh_values(n, b, 0)
                    transpose_probs(n, b, 2)
                    project_out(n, b - 1)
                    weigh_values(n, b, 1)
                    weigh_values(n, b, 2)

                def project_out(n, b):
                    pe.wait_ge(headsT_kept, GROUP * n + b + 1)
                    pe.wait_ge(a_y_kept, GROUP * n + b)
                    for c in range(CHUNKS):
                        mm = product(y_bank[:, 0:FEATURES], headsT_high[:, b % 2, c], headsT_low[:, b % 2, c],
                                     weights_high[:, WO, c], weights_low[:, WO, c], c)
                    mm.then_inc(y_made, 1)

                def body(n, i, first, last):
                    scores(n, 0, 0)
                    scores(n, 0, 1)
                    if not first:
                        transpose_probs(n - 1, 2, 0)
                        transpose_probs(n - 1, 2, 1)
                    scores(n, 0, 2)
                    project_v(n, 0)
                    if not first:
                        weigh_values(n - 1, 2, 0)
                        transpose_probs(n - 1, 2, 2)
                    project_v(n, 1)
                    if not first:
                        weigh_values(n - 1, 2, 1)
                        weigh_values(n - 1, 2, 2)
                    scores(n, 1, 0)
                    scores(n, 1, 1)
                    if not first:
                        attend_and_project(n - 1, 3, between=lambda: scores(n, 1, 2))
                    else:
                        scores(n, 1, 2)
                    scores(n, 2, 0)
                    project_v(n, 2)
                    scores(n, 2, 1)
                    project_v(n, 3)
                    if not first:
                        project_out(n - 1, 3)
                    scores(n, 2, 2)
                    transpose_probs(n, 0, 0)
                    transpose_probs(n, 0, 1)
                    scores(n, 3, 0)
                    weigh_values(n, 0, 0)
                    transpose_probs(n, 0, 2)
                    scores(n, 3, 1)
                    weigh_values(n, 0, 1)
                    weigh_values(n, 0, 2)
                    transpose_probs(n, 1, 0)
                    transpose_probs(n, 1, 1)
                    scores(n, 3, 2)
                    weigh_values(n, 1, 0)
                    transpose_probs(n, 1, 2)
                    weigh_values(n, 1, 1)
                    if not last:
                        transpose_h(n + 1, 0, False)
                        transpose_h(n + 1, 1, False)
                    project_out(n, 0)
                    weigh_values(n, 1, 2)
                    if not last:
                        transpose_h(n + 1, 2, False)
                        project_q(n + 1, 0)
                        project_out(n, 1)
                        project_q(n + 1, 1)
                        project_q(n + 1, 2)
                        for m in range(CHUNKS):
                            project_k(n + 1, m)
                    else:
                        transpose_probs(n, 2, 0)
                        transpose_probs(n, 2, 1)
                        weigh_values(n, 2, 0)
                        transpose_probs(n, 2, 2)
                        project_out(n, 1)
                        weigh_values(n, 2, 1)
                        weigh_values(n, 2, 2)
                        attend_and_project(n, 3)
                        project_out(n, 3)

                n0 = first_group(p)
                for c in range(CHUNKS):
                    transpose_h(n0, c, True)
                for m in range(CHUNKS):
                    project_q(n0, m)
                for m in range(CHUNKS):
                    project_k(n0, m)
                groups_of(pe, p, body)

            def convolution(p):
                WL, WR, WS = range(3)
                pe.wait_ge(weights_split, sum(matrices[:p + 1]))

                def project(n, b, w, to, kept, made):
                    pe.wait_ge(gT_split, GROUP * n + b + 1)
                    pe.wait_ge(kept, GROUP * n + b)
                    for c in range(CHUNKS):
                        mm = product(to[:, 0:FEATURES], gT_high[:, b % 2, c], gT_low[:, b % 2, c],
                                     weights_high[:, w, c], weights_low[:, w, c], c)
                    mm.then_inc(made, 1)

                def transpose_attn(n, b):
                    pe.wait_ge(attn_done, GROUP * n + b + 1)
                    pe.wait_ge(attnT_kept, GROUP * n + b)
                    pe.transpose(attnT_bank[:, 0:128], attn[:], ident).then_inc(attnT_made, 1)

                def transpose_g(n, b):
                    if normalises(p):
                        pe.wait_ge(c_h, GROUP * n + b + 1)
                    else:
                        pe.wait_ge(c_h_loaded[b], 16 * (n - first_group(p)) + 16)
                    pe.wait_ge(gT_rounded, GROUP * n + b)
                    for c in range(CHUNKS):
                        mm = pe.transpose(gT_bank[:, c * 128:(c + 1) * 128], hs[:, b, c * 128:(c + 1) * 128], ident)
                    mm.then_inc(gT_made, 1)

                def gram(n, b):
                    pe.wait_ge(gT_kept, GROUP * n + b + 1)
                    pe.wait_ge(u_exp_done, GROUP * n + b)
                    for c in range(CHUNKS):
                        mm = pe.matmul(u_bank[:, 0:128], gT[:, b % 2, c], gT[:, b % 2, c],
                                       start=c == 0, stop=c == CHUNKS - 1)
                    mm.then_inc(u_made, 1)

                def mix(n, b):
                    pe.wait_ge(mix_kept, GROUP * n + b)
                    pe.wait_ge(attnT_kept, GROUP * n + b + 1)
                    pe.wait_ge(left_kept, GROUP * n + b + 1)
                    pe.matmul(mix_bank[:, 0:FEATURES], attn_leftT[:], left[:], start=True, stop=False)
                    pe.wait_ge(right_kept, GROUP * n + b + 1)
                    pe.matmul(mix_bank[:, 0:FEATURES], attn_rightT[:], right[:], start=False, stop=True
                              ).then_inc(mix_made, 1)

                def body(n, i, first, last):
                    for b in range(GROUP):
                        more = not (last and b == GROUP - 1)
                        n1, b1 = (n, b + 1) if b + 1 < GROUP else (n + 1, 0)
                        project(n, b, WL, left_bank, left_kept, left_made)
                        transpose_attn(n, b)
                        if more:
                            transpose_g(n1, b1)
                        project(n, b, WR, right_bank, right_kept, right_made)
                        if more:
                            gram(n1, b1)
                        project(n, b, WS, own_bank, own_copied, own_made)
                        mix(n, b)

                n0 = first_group(p)
                transpose_g(n0, 0)
                gram(n0, 0)
                groups_of(pe, p, body)

            pe.wait_ge(consts_loaded, 16)
            for p in range(len(PASSES)):
                (attention if is_attention(p) else convolution)(p)
                finish_pass(pe, p)

        @block.scalar
        def _(act):
            def normalise(n, b, ready, rstd_done):
                if b == 0:
                    act.wait_ge(rstd_done, n + 1)
                act.activation(hs[:, b], xs[:, b], ACT.Relu, bias=shift[:, b:b + 1],
                               scale=rstd[:, b:b + 1]).then_inc(ready, 1)

            def round_weights(p):
                act.wait_ge(params_loaded[p], params(p))
                for w in range(matrices[p]):
                    act.copy(flat(weights_high[:, w]), flat(weights[:, w])).then_inc(weights_rounded, 1)

            def attention(p):
                def round_hT(n, c):
                    act.wait_ge(hT_made, CHUNKS * n + c + 1)
                    act.copy(flat(hT_high[:, c]), proj_bank[c % 2][:, :]).then_inc(hT_rounded, 1)

                def keep_q(n, m):
                    act.wait_ge(q_made, CHUNKS * n + m + 1)
                    act.mul(flat(qT[:, m]), proj_bank[(m + 1) % 2][:, :], SCALE).then_inc(q_kept, 1)

                def keep_k(n, m):
                    act.wait_ge(k_made, CHUNKS * n + m + 1)
                    for g in (0, 1):
                        ins = act.copy(kT[g * HEAD:(g + 1) * HEAD, m, :, g],
                                       proj_bank[m % 2][g * HEAD:(g + 1) * HEAD, :].rearrange("p (b n) -> p b n", b=GROUP))
                    ins.then_inc(k_kept_act, 1)

                def exponentials(n, b):
                    act.wait_ge(max_taken, GROUP * n + b + 1)
                    act.activation(probs[:, b], probs[:, b], ACT.Exp).then_inc(exp_done, 1)

                def keep_probsT(n, b, m):
                    t = CHUNKS * b + m
                    act.wait_ge(probsT_made, BANKS_PER_GROUP * n + t + 1)
                    act.copy(flat(probsT[:, m]), probsT_bank[t % 2][:, :]).then_inc(probsT_kept, 1)

                def round_headsT(n, b):
                    act.wait_ge(headsT_made, GROUP * n + b + 1)
                    act.copy(flat(headsT_high[:, b % 2]), headsT_bank[:, 0:FEATURES]).then_inc(headsT_rounded, 1)

                def hold_x(n):
                    act.wait_ge(a_x_loaded, 16 * n + 16)
                    act.wait_ge(res_made, GROUP * n + 2)
                    for b in (2, 3):
                        act.copy(held_x[:, b - 2], xs[:, b]).then_inc(x_held, 1)

                def keep_all_probsT(n, b):
                    for m in range(CHUNKS):
                        keep_probsT(n, b, m)

                def body(n, i, first, last):
                    if not first:
                        keep_all_probsT(n - 1, 2)
                    hold_x(n)
                    if not first:
                        round_headsT(n - 1, 2)
                    if not first:
                        keep_probsT(n - 1, 3, 0)
                        keep_probsT(n - 1, 3, 1)
                    exponentials(n, 0)
                    if not first:
                        keep_probsT(n - 1, 3, 2)
                    if not first:
                        round_headsT(n - 1, 3)
                    exponentials(n, 1)
                    keep_all_probsT(n, 0)
                    if not last:
                        normalise(n + 1, 0, a_h, a_rstd)
                    round_headsT(n, 0)
                    keep_probsT(n, 1, 0)
                    keep_probsT(n, 1, 1)
                    if not last:
                        normalise(n + 1, 1, a_h, a_rstd)
                        normalise(n + 1, 2, a_h, a_rstd)
                        normalise(n + 1, 3, a_h, a_rstd)
                    keep_probsT(n, 1, 2)
                    if not last:
                        for c in range(CHUNKS):
                            round_hT(n + 1, c)
                        round_headsT(n, 1)
                        keep_q(n + 1, 0)
                        exponentials(n, 2)
                        keep_q(n + 1, 1)
                        keep_q(n + 1, 2)
                        exponentials(n, 3)
                        keep_k(n + 1, 0)
                        keep_k(n + 1, 1)
                        keep_k(n + 1, 2)
                    else:
                        exponentials(n, 2)
                        round_headsT(n, 1)
                        exponentials(n, 3)
                        keep_all_probsT(n, 2)
                        round_headsT(n, 2)
                        keep_all_probsT(n, 3)
                        round_headsT(n, 3)

                n0 = first_group(p)
                for b in range(GROUP):
                    normalise(n0, b, a_h, a_rstd)
                for c in range(CHUNKS):
                    round_hT(n0, c)
                for m in range(CHUNKS):
                    keep_q(n0, m)
                for m in range(CHUNKS):
                    keep_k(n0, m)
                groups_of(act, p, body)

            def convolution(p):
                def keep_gT(n, b):
                    act.wait_ge(gT_made, GROUP * n + b + 1)
                    act.copy(flat(gT[:, b % 2]), gT_bank[:, 0:FEATURES]).then_inc(gT_kept, 1)
                    act.copy(flat(gT_high[:, b % 2]), gT_bank[:, 0:FEATURES]).then_inc(gT_rounded, 1)

                def copy_own(n, b):
                    act.wait_ge(own_made, GROUP * n + b + 1)
                    act.wait_ge(mix_kept, GROUP * n + b)
                    act.copy(own[:], own_bank[:, 0:FEATURES]).then_inc(own_copied, 1)

                def exponentials(n, b):
                    act.wait_ge(u_max_found, GROUP * n + b + 1)
                    act.mul(neg_max_scaled[:], neg_max[:], SCALE).then_inc(u_max_scaled, 1)
                    act.wait_ge(u_max_scaled, GROUP * n + b + 1)
                    act.activation(e[:], u_bank[:, 0:128], ACT.Exp, bias=neg_max_scaled[:], scale=SCALE,
                                   accum_out=e_sum[:]).then_inc(u_exp_done, 1)

                def normalise_out(count, b):
                    act.wait_ge(o_rstd_done, count)
                    act.activation(normed[:], mixed[:, b % 2], ACT.Identity, bias=o_shift[:, b % 2:b % 2 + 1],
                                   scale=o_rstd[:, b % 2:b % 2 + 1]).then_inc(o_normed, 1)

                def body(n, i, first, last):
                    for b in range(GROUP):
                        more = not (last and b == GROUP - 1)
                        n1, b1 = (n, b + 1) if b + 1 < GROUP else (n + 1, 0)
                        if more:
                            keep_gT(n1, b1)
                        if b > 0 or not first:
                            normalise_out(GROUP * n + b, (b - 1) % GROUP)
                        if more:
                            exponentials(n1, b1)
                        copy_own(n, b)
                        if b == 2 and not last and normalises(p):
                            for b2 in range(GROUP):
                                normalise(n + 1, b2, c_h, c_rstd)
                    if last:
                        normalise_out(GROUP * n + GROUP, GROUP - 1)

                n0 = first_group(p)
                if normalises(p):
                    for b in range(GROUP):
                        normalise(n0, b, c_h, c_rstd)
                keep_gT(n0, 0)
                exponentials(n0, 0)
                groups_of(act, p, body)

            for p in range(len(PASSES)):
                round_weights(p)
                (attention if is_attention(p) else convolution)(p)
                finish_pass(act, p)

        @block.gpsimd
        def _(pool):
            def reciprocal_deviation(n, var_done, pow_done, rstd_done):
                pool.wait_ge(var_done, n + 1)
                pool.tensor_tensor(rstd[:], var_eps[:], minus_half[:], ALU.pow).then_inc(pow_done, 1)
                pool.wait_ge(pow_done, n + 1)
                pool.tensor_tensor(shift[:], neg_mean[:], rstd[:], ALU.mult).then_inc(rstd_done, 1)

            def attention(p):
                BV, BO = range(2)
                pool.wait_ge(params_loaded[p], params(p))

                def keep_residual(n, b, first):
                    if not first:
                        pool.wait_ge(a_y_kept, GROUP * (n - 1) + b + 1)
                    if b < 2:
                        pool.wait_ge(a_x_loaded, 16 * n + 16)
                        x_of = xs[:, b]
                    else:
                        pool.wait_ge(x_held, 2 * n + b - 1)
                        x_of = held_x[:, b - 2]
                    pool.tensor_tensor(res[:, b], x_of, vector(p, BO), ALU.add).then_inc(res_made, 1)

                def take_max(n, b):
                    pool.wait_ge(abs_found, GROUP * n + b + 1)
                    pool.tensor_tensor(probs[:, b], probs[:, b],
                                       row_max[:, b].unsqueeze(2).to_broadcast([128, HEADS, NODES]),
                                       ALU.subtract).then_inc(max_taken, 1)

                def normalise_probs(n, b):
                    pool.wait_ge(sums_guarded, GROUP * n + b + 1)
                    pool.tensor_tensor(probs[:, b], probs[:, b],
                                       inv_kept[:, b].unsqueeze(2).to_broadcast([128, HEADS, NODES]),
                                       ALU.mult).then_inc(probs_ready, 1)

                def body(n, i, first, last):
                    for b in (0, 1):
                        keep_residual(n, b, first)
                    if not first:
                        normalise_probs(n - 1, 3)
                    take_max(n, 0)
                    take_max(n, 1)
                    normalise_probs(n, 0)
                    normalise_probs(n, 1)
                    if not last:
                        reciprocal_deviation(n + 1, a_var, a_pow, a_rstd)
                    for b in (2, 3):
                        keep_residual(n, b, first)
                    take_max(n, 2)
                    take_max(n, 3)
                    normalise_probs(n, 2)
                    if last:
                        normalise_probs(n, 3)

                reciprocal_deviation(first_group(p), a_var, a_pow, a_rstd)
                groups_of(pool, p, body)

            def convolution(p):
                BL, BR, BS, GAMMA, BETA = range(5)
                pool.wait_ge(params_loaded[p], params(p))

                def add_own_bias(n, b):
                    pool.wait_ge(own_copied, GROUP * n + b + 1)
                    pool.tensor_tensor(own[:], own[:], vector(p, BS), ALU.add).then_inc(own_kept, 1)

                def split_gT(n, b):
                    pool.wait_ge(gT_rounded, GROUP * n + b + 1)
                    pool.tensor_tensor(flat(gT_low[:, b % 2]), flat(gT[:, b % 2]), flat(gT_high[:, b % 2]).bitcast(F32),
                                       ALU.subtract).then_inc(gT_split, 1)

                def out_deviation(count, b):
                    pool.wait_ge(o_var, count)
                    pool.tensor_tensor(o_rstd[:, b % 2:b % 2 + 1], o_var_eps[:], minus_half[:, 0:1], ALU.pow
                                       ).then_inc(o_pow, 1)
                    pool.wait_ge(o_pow, count)
                    pool.tensor_tensor(o_shift[:, b % 2:b % 2 + 1], o_neg_mean[:], o_rstd[:, b % 2:b % 2 + 1],
                                       ALU.mult).then_inc(o_rstd_done, 1)

                def scale_and_shift(count):
                    pool.wait_ge(o_normed, count)
                    pool.tensor_tensor(normed[:], normed[:], vector(p, GAMMA), ALU.mult).then_inc(o_scaled, 1)
                    pool.wait_ge(o_scaled, count)
                    pool.tensor_tensor(normed[:], normed[:], vector(p, BETA), ALU.add).then_inc(o_shifted, 1)

                def body(n, i, first, last):
                    for b in range(GROUP):
                        n1, b1 = (n, b + 1) if b + 1 < GROUP else (n + 1, 0)
                        if b > 0 or not first:
                            out_deviation(GROUP * n + b, (b - 1) % GROUP)
                        if not (last and b == GROUP - 1):
                            split_gT(n1, b1)
                        if b > 0 or not first:
                            scale_and_shift(GROUP * n + b)
                        add_own_bias(n, b)
                        if b == 1 and not last and normalises(p):
                            reciprocal_deviation(n + 1, c_var, c_pow, c_rstd)
                    if last:
                        out_deviation(GROUP * n + GROUP, GROUP - 1)
                        scale_and_shift(GROUP * n + GROUP)

                if normalises(p):
                    reciprocal_deviation(first_group(p), c_var, c_pow, c_rstd)
                split_gT(first_group(p), 0)
                groups_of(pool, p, body)

            pool.memset(minus_half[:], -0.5)
            pool.memset(kT[:], 0.0)
            pool.memset(values[:], 0.0).then_inc(consts_set, 1)
            for p in range(len(PASSES)):
                (attention if is_attention(p) else convolution)(p)
                finish_pass(pool, p)

        @block.vector
        def _(dve):
            def wait_in_memset(sem_, value):
                dve.wait_ge(sem_, value)
                dve.memset(spare[:], 0.0)

            def split_weights(p):
                dve.wait_ge(params_loaded[p], params(p))
                for w in range(matrices[p]):
                    dve.wait_ge(weights_rounded, sum(matrices[:p]) + w + 1)
                    dve.tensor_tensor(flat(weights_low[:, w]), flat(weights[:, w]), flat(weights_high[:, w]).bitcast(F32),
                                      ALU.subtract).then_inc(weights_split, 1)

            def moments_of(n, loaded, bn, mv, var):
                dve.wait_ge(loaded, 16 * n + 16)
                for b in range(GROUP):
                    ins = dve.bn_stats(stats[:, b], xs[:, b])
                ins.then_inc(bn, 1)
                wait_in_memset(bn, n + 1)
                for b in range(GROUP):
                    ins = dve.bn_aggr(moments[:, b], stats[:, b])
                ins.then_inc(mv, 1)
                dve.wait_ge(mv, n + 1)
                dve.tensor_scalar(neg_mean[:], moments[:, :, 0], -1.0, None, ALU.mult)
                dve.tensor_scalar(var_eps[:], moments[:, :, 1], EPS_IN, None, ALU.add).then_inc(var, 1)

            def attention(p):
                BV, BO = range(2)
                n0 = first_group(p)

                def split_hT(n, c):
                    dve.wait_ge(hT_rounded, CHUNKS * n + c + 1)
                    dve.tensor_tensor(flat(hT_low[:, c]), proj_bank[c % 2][:, :], flat(hT_high[:, c]).bitcast(F32),
                                      ALU.subtract).then_inc(hT_kept, 1)

                def keep_k(n, m):
                    dve.wait_ge(k_made, CHUNKS * n + m + 1)
                    for g in (2, 3):
                        ins = dve.tensor_copy(kT[g * HEAD:(g + 1) * HEAD, m, :, g],
                                              proj_bank[m % 2][g * HEAD:(g + 1) * HEAD, :]
                                              .rearrange("p (b n) -> p b n", b=GROUP))
                    ins.then_inc(k_kept_dve, 1)

                def split_headsT(n, b):
                    dve.wait_ge(headsT_rounded, GROUP * n + b + 1)
                    dve.tensor_tensor(flat(headsT_low[:, b % 2]), headsT_bank[:, 0:FEATURES],
                                      flat(headsT_high[:, b % 2]).bitcast(F32), ALU.subtract).then_inc(headsT_kept, 1)

                def keep_v(n, b):
                    dve.wait_ge(v_made, GROUP * n + b + 1)
                    dve.tensor_tensor(values[:, b, :, 0:HEAD],
                                      proj_bank[b % 2][:, 0:FEATURES].rearrange("p (h w) -> p h w", w=HEAD),
                                      vector(p, BV).rearrange("p (h w) -> p h w", w=HEAD), ALU.add).then_inc(v_kept, 1)

                def add_bias(n, b, m):
                    if b == 0 and m == 0:
                        dve.wait_ge(a_adj_loaded, 16 * n + 16)
                    t = CHUNKS * b + m
                    dve.wait_ge(scores_made, BANKS_PER_GROUP * n + t + 1)
                    dve.scalar_tensor_tensor(
                        out=probs[:, b, m * PER_CHUNK:(m + 1) * PER_CHUNK],
                        in0=adj[:, b].unsqueeze(1).to_broadcast([128, PER_CHUNK, NODES]),
                        scalar=BIAS_TIMES[PASSES[p]],
                        in1=score_bank[t % 2][:, :].rearrange("p (g n) -> p g n", g=PER_CHUNK),
                        op0=ALU.mult, op1=ALU.add).then_inc(scores_kept, 1)

                def find_max(n, b):
                    dve.wait_ge(scores_kept, BANKS_PER_GROUP * n + CHUNKS * b + CHUNKS)
                    dve.tensor_reduce(row_max[:, b], probs[:, b], AX.X, ALU.max).then_inc(max_found, 1)

                def find_abs(n, b):
                    dve.tensor_reduce(row_abs[:, b], probs[:, b], AX.X, ALU.max, apply_absolute_value=True
                                      ).then_inc(abs_found, 1)

                def invert_sums(n, b):
                    dve.wait_ge(exp_done, GROUP * n + b + 1)
                    dve.tensor_reduce(row_sum[:, b], probs[:, b], AX.X, ALU.add).then_inc(sums_found, 1)
                    dve.wait_ge(sums_found, GROUP * n + b + 1)
                    dve.reciprocal(inv_sum[:, b], row_sum[:, b]).then_inc(sums_inverted, 1)
                    dve.wait_ge(sums_inverted, GROUP * n + b + 1)
                    dve.scalar_tensor_tensor(out=inv_kept[:, b], in0=row_abs[:, b], scalar=0.0, in1=inv_sum[:, b],
                                             op0=ALU.is_gt, op1=ALU.mult).then_inc(sums_guarded, 1)

                def keep_y(n, b):
                    dve.wait_ge(a_y_stored[b // 2], 16 * n)
                    dve.wait_ge(res_made, GROUP * n + b + 1)
                    dve.wait_ge(y_made, GROUP * n + b + 1)
                    dve.tensor_tensor(ys[:, b], y_bank[:, 0:FEATURES], res[:, b], ALU.add).then_inc(a_y_kept, 1)

                def body(n, i, first, last):
                    for m in range(CHUNKS):
                        add_bias(n, 0, m)
                    if not first:
                        invert_sums(n - 1, 3)
                    keep_v(n, 0)
                    find_max(n, 0)
                    find_abs(n, 0)
                    keep_v(n, 1)
                    if not first:
                        split_headsT(n - 1, 2)
                    for m in range(CHUNKS):
                        add_bias(n, 1, m)
                    find_max(n, 1)
                    find_abs(n, 1)
                    invert_sums(n, 0)
                    if not first:
                        keep_y(n - 1, 2)
                        split_headsT(n - 1, 3)
                    add_bias(n, 2, 0)
                    keep_v(n, 2)
                    add_bias(n, 2, 1)
                    keep_v(n, 3)
                    invert_sums(n, 1)
                    add_bias(n, 2, 2)
                    if not first:
                        keep_y(n - 1, 3)
                    if not last:
                        moments_of(n + 1, a_x_loaded, a_bn, a_mv, a_var)
                    add_bias(n, 3, 0)
                    split_headsT(n, 0)
                    add_bias(n, 3, 1)
                    find_max(n, 2)
                    add_bias(n, 3, 2)
                    find_abs(n, 2)
                    if not last:
                        split_hT(n + 1, 0)
                        split_hT(n + 1, 1)
                    keep_y(n, 0)
                    if not last:
                        split_hT(n + 1, 2)
                        split_headsT(n, 1)
                    find_max(n, 3)
                    if not last:
                        find_abs(n, 3)
                        keep_y(n, 1)
                        invert_sums(n, 2)
                        for m in range(CHUNKS):
                            keep_k(n + 1, m)
                    else:
                        find_abs(n, 3)
                        invert_sums(n, 2)
                        split_headsT(n, 1)
                        invert_sums(n, 3)
                        keep_y(n, 1)
                        split_headsT(n, 2)
                        keep_y(n, 2)
                        split_headsT(n, 3)
                        keep_y(n, 3)

                moments_of(n0, a_x_loaded, a_bn, a_mv, a_var)
                split_weights(p)
                for c in range(CHUNKS):
                    split_hT(n0, c)
                for m in range(CHUNKS):
                    keep_k(n0, m)
                groups_of(dve, p, body)

            def convolution(p):
                BL, BR, BS, GAMMA, BETA = range(5)
                n0 = first_group(p)
                residuals = 0 if p == 1 else -GROUPS

                def keep_side(n, b, to, bank_, v, made, kept):
                    dve.wait_ge(made, GROUP * n + b + 1)
                    dve.tensor_tensor(to[:], bank_[:, 0:FEATURES], vector(p, v), ALU.add).then_inc(kept, 1)

                def split_attn(n, b):
                    dve.wait_ge(attnT_made, GROUP * n + b + 1)
                    dve.tensor_tensor(attn_leftT[:], attnT_bank[:, 0:128], later, ALU.mult)
                    dve.tensor_tensor(attn_rightT[:], attnT_bank[:, 0:128], earlier, ALU.mult).then_inc(attnT_kept, 1)

                def find_max(n, b):
                    dve.wait_ge(u_made, GROUP * n + b + 1)
                    dve.tensor_reduce(neg_max[:], u_bank[:, 0:128], AX.X, ALU.max, negate=True).then_inc(u_max_found, 1)

                def attention_rows(n, b):
                    dve.wait_ge(c_adj_loaded[b], 16 * n + 16)
                    dve.wait_ge(u_exp_done, GROUP * n + b + 1)
                    dve.tensor_tensor_reduce(out=e_adj[:], in0=e[:], in1=adj[:, b], scale=1.0, scalar=0.0,
                                             op0=ALU.mult, op1=ALU.add, accum_out=e_adj_sum[:]).then_inc(e_adj_done, 1)
                    dve.wait_ge(e_adj_done, GROUP * n + b + 1)
                    dve.scalar_tensor_tensor(out=denom[:], in0=e_sum[:], scalar=EPS_SUM, in1=e_adj_sum[:],
                                             op0=ALU.mult, op1=ALU.add).then_inc(denom_done, 1)
                    dve.wait_ge(denom_done, GROUP * n + b + 1)
                    dve.reciprocal(inv_denom[:], denom[:]).then_inc(denom_inverted, 1)
                    dve.wait_ge(denom_inverted, GROUP * n + b + 1)
                    dve.tensor_scalar(attn[:], e_adj[:], inv_denom[:], None, ALU.mult).then_inc(attn_done, 1)
                    dve.wait_ge(attn_done, GROUP * n + b + 1)
                    dve.tensor_tensor_reduce(out=attn_ident[:], in0=attn[:], in1=ident, scale=1.0, scalar=0.0,
                                             op0=ALU.mult, op1=ALU.add, accum_out=diag[:, b % 2:b % 2 + 1]
                                             ).then_inc(diag_done, 1)

                def mix_own(n, b):
                    dve.wait_ge(own_kept, GROUP * n + b + 1)
                    dve.wait_ge(diag_done, GROUP * n + b + 1)
                    dve.wait_ge(mix_made, GROUP * n + b + 1)
                    dve.scalar_tensor_tensor(out=mixed[:, b % 2], in0=own[:], scalar=diag[:, b % 2:b % 2 + 1],
                                             in1=mix_bank[:, 0:FEATURES], op0=ALU.mult, op1=ALU.add
                                             ).then_inc(mix_kept, 1)
                    dve.wait_ge(mix_kept, GROUP * n + b + 1)
                    dve.bn_stats(o_stats[:], mixed[:, b % 2]).then_inc(o_bn, 1)
                    wait_in_memset(o_bn, GROUP * n + b + 1)
                    dve.bn_aggr(o_moments[:], o_stats[:]).then_inc(o_mv, 1)
                    dve.wait_ge(o_mv, GROUP * n + b + 1)
                    dve.tensor_scalar(o_neg_mean[:], o_moments[:, 0:1], -1.0, None, ALU.mult)
                    dve.tensor_scalar(o_var_eps[:], o_moments[:, 1:2], EPS_OUT, None, ALU.add).then_inc(o_var, 1)

                def keep_y(n, b, count):
                    dve.wait_ge(c_y_stored[b], 16 * n)
                    if residual[p] is not None:
                        dve.wait_ge(c_res_loaded[b], 16 * (n + residuals) + 16)
                    dve.wait_ge(o_shifted, count)
                    if residual[p] is not None:
                        dve.scalar_tensor_tensor(out=ys[:, b], in0=normed[:], scalar=0.0, in1=res[:, b],
                                                 op0=ALU.max, op1=ALU.add).then_inc(c_y_kept, 1)
                    else:
                        dve.tensor_scalar(ys[:, b], normed[:], 0.0, None, ALU.max).then_inc(c_y_kept, 1)

                def body(n, i, first, last):
                    for b in range(GROUP):
                        more = not (last and b == GROUP - 1)
                        n1, b1 = (n, b + 1) if b + 1 < GROUP else (n + 1, 0)
                        keep_side(n, b, left, left_bank, BL, left_made, left_kept)
                        split_attn(n, b)
                        keep_side(n, b, right, right_bank, BR, right_made, right_kept)
                        if b == 1 and not last and normalises(p):
                            moments_of(n + 1, c_x_loaded, c_bn, c_mv, c_var)
                        if more:
                            find_max(n1, b1)
                            attention_rows(n1, b1)
                        if b > 0:
                            keep_y(n, b - 1, GROUP * n + b)
                        elif not first:
                            keep_y(n - 1, GROUP - 1, GROUP * n)
                        mix_own(n, b)
                    if last:
                        keep_y(n, GROUP - 1, GROUP * n + GROUP)

                if normalises(p):
                    moments_of(n0, c_x_loaded, c_bn, c_mv, c_var)
                split_weights(p)
                find_max(n0, 0)
                attention_rows(n0, 0)
                groups_of(dve, p, body)

            dve.wait_ge(consts_set, 1)
            dve.wait_ge(consts_loaded, 16)
            for p in range(len(PASSES)):
                (attention if is_attention(p) else convolution)(p)
                finish_pass(dve, p)


def kernel(x, adj, L0_gnn_Wq, L0_gnn_Wk, L0_gnn_Wv, L0_gnn_bv, L0_gnn_Wo, L0_gnn_bo, L1_gnn_W_left, L1_gnn_b_left,
           L1_gnn_W_self, L1_gnn_b_self, L1_gnn_W_right, L1_gnn_b_right, L1_gnn_gamma, L1_gnn_beta, L2_gnn_Wl,
           L2_gnn_bl, L2_gnn_Ws, L2_gnn_bs, L2_gnn_Wr, L2_gnn_br, L2_gnn_ln_w, L2_gnn_ln_b, L3_gnn_Wq, L3_gnn_Wk,
           L3_gnn_Wv, L3_gnn_bv, L3_gnn_Wo, L3_gnn_bo):
    import numpy as np
    import concourse.bacc as bacc
    from concourse.bass_utils import run_bass_kernel_spmd

    nc = bacc.Bacc("TRN2", target_bir_lowering=False, num_devices=1)
    arrays = {}

    def give(name, a):
        arrays[name] = np.ascontiguousarray(a)
        return nc.dram_tensor(name, arrays[name].shape, mybir.dt.from_np(arrays[name].dtype),
                              kind="ExternalInput").ap()

    row, column = np.indices((128, 128))
    consts = np.stack([row == column, row > column, row < column], axis=1).astype(np.float32)
    weights = (
        (L0_gnn_Wq, L0_gnn_Wk, L0_gnn_Wv, L0_gnn_Wo),
        (L1_gnn_W_left, L1_gnn_W_right, L1_gnn_W_self),
        (L2_gnn_Wl[0], L2_gnn_Wr[0], L2_gnn_Ws[0]),
        (L2_gnn_Wl[1], L2_gnn_Wr[1], L2_gnn_Ws[1]),
        (L3_gnn_Wq, L3_gnn_Wk, L3_gnn_Wv, L3_gnn_Wo),
    )
    vectors = (
        (L0_gnn_bv, L0_gnn_bo),
        (L1_gnn_b_left, L1_gnn_b_right, L1_gnn_b_self, L1_gnn_gamma, L1_gnn_beta),
        (L2_gnn_bl[0], L2_gnn_br[0], L2_gnn_bs[0], L2_gnn_ln_w[0], L2_gnn_ln_b[0]),
        (L2_gnn_bl[1], L2_gnn_br[1], L2_gnn_bs[1], L2_gnn_ln_w[1], L2_gnn_ln_b[1]),
        (L3_gnn_bv, L3_gnn_bo),
    )
    weight_aps = [[give(f"weight{p}_{w}", np.asarray(m).T) for w, m in enumerate(ms)] for p, ms in enumerate(weights)]
    vector_aps = [[give(f"vector{p}_{v}", np.asarray(m)) for v, m in enumerate(vs)] for p, vs in enumerate(vectors)]
    x_ap, adj_ap, consts_ap = give("x_in", x), give("adj_in", adj), give("consts_in", consts)
    out = nc.dram_tensor("y_out", (GRAPHS, NODES, FEATURES), F32, kind="ExternalOutput").ap()
    build(nc, x_ap, adj_ap, consts_ap, weight_aps, vector_aps, out)
    return run_bass_kernel_spmd(nc, [arrays], core_ids=[0]).results[0]["y_out"]
```

```python
from contextlib import ExitStack

import concourse.bass as bass
from concourse import mybir

F32 = mybir.dt.float32
F32R = mybir.dt.float32r
ALU = mybir.AluOpType
ACT = mybir.ActivationFunctionType
AX = mybir.AxisListType

GRAPHS, NODES, FEATURES, HEADS = 64, 128, 384, 12
HEAD = FEATURES // HEADS
CHUNKS = FEATURES // 128
PER_CHUNK = HEADS // CHUNKS
GROUP = 4
GROUPS = GRAPHS // GROUP
BANKS_PER_GROUP = GROUP * CHUNKS
SCALE = float(FEATURES) ** -0.5
EPS_IN, EPS_OUT, EPS_SUM = 1e-5, 1e-12, 1e-10
BIAS_TIMES = {"attention0": 2.0, "attention3": 1.0}
PASSES = ("attention0", "convolution1", "convolution2a", "convolution2b", "attention3")
WEIGHTS, VECTORS = 4, 5


def build(nc, x_in, adj_in, consts_in, weights_in, vectors_in, out):
    x1 = nc.dram_tensor("x_after_0", [GRAPHS, NODES, FEATURES], F32, kind="Internal").ap()
    x2 = nc.dram_tensor("x_after_1", [GRAPHS, NODES, FEATURES], F32, kind="Internal").ap()
    h2 = nc.dram_tensor("h_inside_2", [GRAPHS, NODES, FEATURES], F32, kind="Internal").ap()
    x3 = nc.dram_tensor("x_after_2", [GRAPHS, NODES, FEATURES], F32, kind="Internal").ap()
    source = (x_in, x1, x2, h2, x3)
    residual = (x_in, x1, None, x2, x3)
    target = (x1, x2, h2, x3, out)

    with ExitStack() as ctx:
        def sb(name, shape, dtype=F32):
            return ctx.enter_context(nc.sbuf_tensor(name, shape, dtype))

        def sem(name):
            return ctx.enter_context(nc.semaphore(name))

        consts = sb("consts", [128, 3, 128])
        ident = consts[:, 0, :]
        later = consts[:, 1, :]
        earlier = consts[:, 2, :]
        minus_half = sb("minus_half", [128, GROUP])
        weights = sb("weights", [128, WEIGHTS, CHUNKS, FEATURES])
        weights_high = sb("weights_high", [128, WEIGHTS, CHUNKS, FEATURES], F32R)
        weights_low = sb("weights_low", [128, WEIGHTS, CHUNKS, FEATURES], F32R)
        vectors = sb("vectors", [128, 2, VECTORS, FEATURES])
        xs = sb("xs", [128, GROUP, FEATURES])
        held_x = sb("held_x", [128, GROUP // 2, FEATURES])
        res = sb("res", [128, GROUP, FEATURES])
        ys = sb("ys", [128, GROUP, FEATURES])
        hs = sb("hs", [128, GROUP, FEATURES])
        adj = sb("adj", [128, GROUP, NODES])
        stats = sb("stats", [128, GROUP, 6])
        moments = sb("moments", [128, GROUP, 2])
        var_eps = sb("var_eps", [128, GROUP])
        neg_mean = sb("neg_mean", [128, GROUP])
        rstd = sb("rstd", [128, GROUP])
        shift = sb("shift", [128, GROUP])
        spare = sb("spare", [128, 1])
        hT_high = sb("hT_high", [128, CHUNKS, GROUP, NODES], F32R)
        hT_low = sb("hT_low", [128, CHUNKS, GROUP, NODES], F32R)
        qT = sb("qT", [128, CHUNKS, GROUP, NODES])
        kT = sb("kT", [128, CHUNKS, GROUP, PER_CHUNK, NODES])
        values = sb("values", [128, GROUP, HEADS, 128])
        probs = sb("probs", [128, GROUP, HEADS, NODES])
        probsT = sb("probsT", [128, CHUNKS, PER_CHUNK, NODES])
        row_max = sb("row_max", [128, GROUP, HEADS])
        row_abs = sb("row_abs", [128, GROUP, HEADS])
        row_sum = sb("row_sum", [128, GROUP, HEADS])
        inv_sum = sb("inv_sum", [128, GROUP, HEADS])
        inv_kept = sb("inv_kept", [128, GROUP, HEADS])
        headsT_high = sb("headsT_high", [128, 2, CHUNKS, NODES], F32R)
        headsT_low = sb("headsT_low", [128, 2, CHUNKS, NODES], F32R)
        scratch = probs[:].rearrange("p b h n -> p (b h n)")
        left, right, own, normed = (scratch[:, k * FEATURES:(k + 1) * FEATURES] for k in range(4))
        mixed = scratch[:, 4 * FEATURES:6 * FEATURES].rearrange("p (b d) -> p b d", b=2)
        gT = scratch[:, 6 * FEATURES:8 * FEATURES].rearrange("p (b c n) -> p b c n", b=2, c=CHUNKS)
        e, e_adj, attn, attn_ident, attn_leftT, attn_rightT = (
            scratch[:, 8 * FEATURES + k * NODES:8 * FEATURES + (k + 1) * NODES] for k in range(6))
        gT_high = hT_high[:].rearrange("p c b n -> p (c b) n")[:, 0:2 * CHUNKS].rearrange("p (b c) n -> p b c n", b=2)
        gT_low = hT_low[:].rearrange("p c b n -> p (c b) n")[:, 0:2 * CHUNKS].rearrange("p (b c) n -> p b c n", b=2)
        neg_max = sb("neg_max", [128, 1])
        neg_max_scaled = sb("neg_max_scaled", [128, 1])
        e_sum = sb("e_sum", [128, 1])
        e_adj_sum = sb("e_adj_sum", [128, 1])
        denom = sb("denom", [128, 1])
        inv_denom = sb("inv_denom", [128, 1])
        diag = sb("diag", [128, 2])
        o_stats = sb("o_stats", [128, 6])
        o_moments = sb("o_moments", [128, 2])
        o_var_eps = sb("o_var_eps", [128, 1])
        o_neg_mean = sb("o_neg_mean", [128, 1])
        o_rstd = sb("o_rstd", [128, 2])
        o_shift = sb("o_shift", [128, 2])

        bank = [ctx.enter_context(nc.psum_tensor(f"bank{i}", [128, 512], F32)) for i in range(8)]
        proj_bank, score_bank, probsT_bank = bank[0:2], bank[2:4], bank[4:6]
        headsT_bank, y_bank = bank[6], bank[7]
        left_bank, right_bank, own_bank, attnT_bank, gT_bank, u_bank, mix_bank = bank[0:7]

        consts_loaded = sem("consts_loaded")
        keys_zeroed, values_zeroed = sem("keys_zeroed"), sem("values_zeroed")
        weight_loaded = [sem(f"weight_loaded{w}") for w in range(WEIGHTS)]
        vectors_loaded = [sem(f"vectors_loaded{p}") for p in range(len(PASSES))]
        pass_done = sem("pass_done")
        weights_rounded, weights_split = sem("weights_rounded"), sem("weights_split")
        x_loaded, h_made = sem("x_loaded"), sem("h_made")
        bn_done, mv_done, var_done, pow_done, rstd_done = (
            sem("bn_done"), sem("mv_done"), sem("var_done"), sem("pow_done"), sem("rstd_done"))
        a_adj_loaded, x_held = sem("a_adj_loaded"), sem("x_held")
        a_y_stored = [sem(f"a_y_stored{half}") for half in range(2)]
        hT_made, hT_rounded, hT_kept = sem("hT_made"), sem("hT_rounded"), sem("hT_kept")
        q_made, q_kept = sem("q_made"), sem("q_kept")
        k_made, k_kept_act, k_kept_dve = sem("k_made"), sem("k_kept_act"), sem("k_kept_dve")
        v_made, v_kept = sem("v_made"), sem("v_kept")
        scores_made, scores_kept = sem("scores_made"), sem("scores_kept")
        max_found, abs_found, max_taken, exp_done = sem("max_found"), sem("abs_found"), sem("max_taken"), sem("exp_done")
        sums_found, sums_inverted, sums_guarded, probs_ready = sem("sums_found"), sem("sums_inverted"), sem("sums_guarded"), sem("probs_ready")
        probsT_made, probsT_kept = sem("probsT_made"), sem("probsT_kept")
        headsT_made, headsT_rounded, headsT_kept = sem("headsT_made"), sem("headsT_rounded"), sem("headsT_kept")
        y_made, a_y_kept, res_made = sem("y_made"), sem("a_y_kept"), sem("res_made")
        c_h_loaded = [sem(f"c_h_loaded{b}") for b in range(GROUP)]
        c_adj_loaded = [sem(f"c_adj_loaded{b}") for b in range(GROUP)]
        c_res_loaded = [sem(f"c_res_loaded{b}") for b in range(GROUP)]
        c_y_stored = [sem(f"c_y_stored{b}") for b in range(GROUP)]
        gT_made, gT_kept, gT_rounded = sem("gT_made"), sem("gT_kept"), sem("gT_rounded")
        gT_split, u_made = sem("gT_split"), sem("u_made")
        left_made, left_kept = sem("left_made"), sem("left_kept")
        right_made, right_kept = sem("right_made"), sem("right_kept")
        own_made, own_copied, own_kept = sem("own_made"), sem("own_copied"), sem("own_kept")
        u_max_found, u_max_scaled, u_exp_done = sem("u_max_found"), sem("u_max_scaled"), sem("u_exp_done")
        e_adj_done, denom_done, denom_inverted = sem("e_adj_done"), sem("denom_done"), sem("denom_inverted")
        attn_done, diag_done, attnT_made, attnT_kept = (
            sem("attn_done"), sem("diag_done"), sem("attnT_made"), sem("attnT_kept"))
        mix_made, mix_kept = sem("mix_made"), sem("mix_kept")
        o_bn, o_mv, o_var, o_pow, o_rstd_done = (
            sem("o_bn"), sem("o_mv"), sem("o_var"), sem("o_pow"), sem("o_rstd_done"))
        o_normed, o_scaled, o_shifted, c_y_kept = (
            sem("o_normed"), sem("o_scaled"), sem("o_shifted"), sem("c_y_kept"))

        matrices = [len(ms) for ms in weights_in]

        def loads_of_weight(p, w):
            return 16 * sum(1 for count in matrices[:p + 1] if w < count)

        def splits_of_weight(p, w):
            return sum(matrices[:p]) + w + 1

        def flat(ap):
            return ap.rearrange("p a b -> p (a b)")

        def vector(p, v):
            return vectors[:, p % 2, v, :]

        def goes_on(p):
            return 0 <= p < len(PASSES) - 1 and PASSES[p].startswith("convolution") and PASSES[p + 1].startswith("convolution")

        def meets_attention(p):
            return 0 <= p < len(PASSES) - 1 and PASSES[p].startswith("convolution") and not goes_on(p)

        def needs_barrier(p):
            return not goes_on(p) and not meets_attention(p)

        def finish_pass(eng, p):
            if needs_barrier(p):
                eng.drain().then_inc(pass_done, 1)
                eng.wait_ge(pass_done, 5 * sum(1 for q in range(p + 1) if needs_barrier(q)))

        def after(p, n, b, last):
            n1, b1 = (n, b + 1) if b + 1 < GROUP else (n + 1, 0)
            ends = last and b == GROUP - 1
            return not ends or goes_on(p), n1, b1, p + 1 if ends and goes_on(p) else p

        def before(p, b, first):
            starts = first and b == 0
            return not starts or goes_on(p - 1), (b - 1) % GROUP, p - 1 if starts else p

        def first_group(p):
            return GROUPS if PASSES[p] == "attention3" else 0 if p == 0 else GROUPS * (p - 1)

        def is_attention(p):
            return PASSES[p].startswith("attention")

        def normalises(p):
            return PASSES[p] != "convolution2b"

        def normalised(p, n):
            return n - first_group(p) + GROUPS * sum(1 for q in range(p) if normalises(q))

        def next_normalised(p, n, last):
            if not last:
                return normalised(p, n + 1) if normalises(p) else None
            more = p + 1 < len(PASSES) and normalises(p + 1)
            return normalised(p + 1, first_group(p + 1)) if more else None

        def groups_of(eng, p, body):
            n0 = first_group(p)
            body(n0, 0, True, False)
            with eng.Fori(1, GROUPS - 1) as i:
                body(i + n0, i, False, False)
            body(n0 + GROUPS - 1, GROUPS - 1, False, True)

        block = ctx.enter_context(nc.Block())

        @block.sync
        def _(sp):
            def graphs(dram, i):
                return dram[bass.ts(i, GROUP)].rearrange("b n d -> n b d")

            def graph(dram, i, b):
                return dram[bass.ds(i * GROUP + b, 1)].rearrange("b n d -> (b n) d")

            def load_weight(p, w):
                sp.dma_start(weights[:, w], weights_in[p][w].rearrange("(c k) n -> k c n", k=128)
                             ).then_inc(weight_loaded[w], 16)

            def load_vectors(p):
                for v, vec in enumerate(vectors_in[p]):
                    sp.dma_start(vector(p, v), vec.partition_broadcast(128)).then_inc(vectors_loaded[p], 16)

            def load_next_params(p):
                if p + 1 < len(PASSES):
                    sp.wait_ge(weights_split, sum(matrices[:p + 1]))
                    for w in range(matrices[p + 1]):
                        load_weight(p + 1, w)
                    load_vectors(p + 1)

            def wait_stored(p, groups):
                stored = a_y_stored if is_attention(p) else c_y_stored
                for s in stored:
                    sp.wait_ge(s, 16 * (first_group(p) + groups))

            def load_x(p, i, last):
                if last:
                    wait_stored(p, 1)
                    sp.dma_start(xs[:], graphs(source[p + 1], 0)).then_inc(x_loaded, 16)
                else:
                    sp.dma_start(xs[:], graphs(source[p], i + 1)).then_inc(x_loaded, 16)

            def load_adj(i):
                sp.dma_start(adj[:], graphs(adj_in, i)).then_inc(a_adj_loaded, 16)

            def load_adj_of_graph(i, b):
                sp.dma_start(adj[:, b], graph(adj_in, i, b)).then_inc(c_adj_loaded[b], 16)

            def attention(p):
                load_next_params(p)
                if p > 0:
                    wait_stored(p - 1, GROUPS)
                pairs = target[p].rearrange("(i h b) n d -> h n i b d", h=2, b=2)

                def store(n, i, half):
                    sp.wait_ge(a_y_kept, GROUP * n + 2 * half + 2)
                    sp.dma_start(pairs[half, :, i], ys[:, 2 * half:2 * half + 2]).then_inc(a_y_stored[half], 16)

                def body(n, i, first, last):
                    if next_normalised(p, n, last) is not None:
                        sp.wait_ge(x_held, 2 * n + 2)
                        load_x(p, i, last)
                    if not first:
                        store(n - 1, i - 1, 1)
                    if not last or p + 1 < len(PASSES):
                        sp.wait_ge(scores_kept, BANKS_PER_GROUP * n + BANKS_PER_GROUP)
                    if not last:
                        load_adj(i + 1)
                    elif p + 1 < len(PASSES):
                        for b in range(GROUP):
                            load_adj_of_graph(0, b)
                    store(n, i, 0)
                    if last:
                        store(n, i, 1)

                groups_of(sp, p, body)

            def convolution(p):
                if residual[p] is not None:
                    for b in range(GROUP):
                        sp.dma_start(res[:, b], graph(residual[p], 0, b)).then_inc(c_res_loaded[b], 16)
                if goes_on(p - 1):
                    wait_stored(p - 1, GROUPS - 1)
                else:
                    load_next_params(p)
                    wait_stored(p - 1, GROUPS)

                def store(of, i, b, count, more):
                    sp.wait_ge(c_y_kept, count)
                    sp.dma_start(graph(target[of], i, b), ys[:, b]).then_inc(c_y_stored[b], 16)
                    if more and residual[p] is not None:
                        sp.dma_start(res[:, b], graph(residual[p], i + 1, b)).then_inc(c_res_loaded[b], 16)

                def body(n, i, first, last):
                    following = next_normalised(p, n, last)
                    if following is not None:
                        sp.wait_ge(h_made, GROUP * following)
                        load_x(p, i, last)
                    for b in range(GROUP):
                        sp.wait_ge(e_adj_done, GROUP * n + b + 1)
                        if not last:
                            load_adj_of_graph(i + 1, b)
                        elif not is_attention(p + 1):
                            load_adj_of_graph(0, b)
                        elif b == GROUP - 1:
                            load_adj(0)
                        if not last and not normalises(p):
                            sp.wait_ge(gT_made, GROUP * n + b + 1)
                            sp.dma_start(hs[:, b], graph(source[p], i + 1, b)).then_inc(c_h_loaded[b], 16)
                        if last and not normalises(p + 1):
                            sp.wait_ge(gT_made, GROUP * n + b + 1)
                            sp.wait_ge(c_y_stored[b], 16 * (first_group(p) + 1))
                            sp.dma_start(hs[:, b], graph(source[p + 1], 0, b)).then_inc(c_h_loaded[b], 16)
                        if b > 0:
                            store(p, i, b - 1, GROUP * n + b, not last)
                        elif not first:
                            store(p, i - 1, GROUP - 1, GROUP * n, True)
                        elif goes_on(p - 1):
                            store(p - 1, GROUPS - 1, GROUP - 1, GROUP * n, False)
                            load_next_params(p)
                            wait_stored(p - 1, GROUPS)
                    if last and not goes_on(p):
                        store(p, i, GROUP - 1, GROUP * n + GROUP, False)

                groups_of(sp, p, body)

            sp.dma_start(xs[:], graphs(x_in, 0)).then_inc(x_loaded, 16)
            sp.dma_start(consts[:], consts_in).then_inc(consts_loaded, 16)
            for w in range(matrices[0]):
                load_weight(0, w)
                if w == 1:
                    load_adj(0)
            load_vectors(0)
            for p in range(len(PASSES)):
                (attention if is_attention(p) else convolution)(p)
                finish_pass(sp, p)
            wait_stored(len(PASSES) - 1, GROUPS)

        @block.tensor
        def _(pe):
            def product(to, left_high, left_low, right_high, right_low, c):
                pe.matmul(to, left_high, right_high, start=c == 0, stop=False)
                pe.matmul(to, left_high, right_low, start=False, stop=False)
                return pe.matmul(to, left_low, right_high, start=False, stop=c == CHUNKS - 1)

            def attention(p):
                WQ, WK, WV, WO = range(4)

                def transpose_h(n, c, first):
                    if c == 0:
                        pe.wait_ge(h_made, GROUP * normalised(p, n) + GROUP)
                    if c < 2 and not first:
                        pe.wait_ge(v_kept, GROUP * n - GROUP + 3 + c)
                    if c == 2:
                        pe.wait_ge(hT_kept, CHUNKS * n + 1)
                    for b in range(GROUP):
                        mm = pe.transpose(proj_bank[c % 2][:, b * 128:(b + 1) * 128],
                                          hs[:, b, c * 128:(c + 1) * 128], ident)
                    mm.then_inc(hT_made, 1)

                def project_chunk(n, w, m, to, made):
                    at = slice(m * 128, (m + 1) * 128)
                    for c in range(CHUNKS):
                        if w == WQ and m == 0:
                            pe.wait_ge(hT_kept, CHUNKS * n + c + 1)
                        mm = product(to[:, :], weights_high[:, w, c, at], weights_low[:, w, c, at],
                                     hT_high[:, c], hT_low[:, c], c)
                    mm.then_inc(made, 1)

                def project_q(n, m):
                    if m == 0:
                        pe.wait_ge(hT_kept, CHUNKS * n + 2)
                    elif m == 2:
                        pe.wait_ge(q_kept, CHUNKS * n + 1)
                    project_chunk(n, WQ, m, proj_bank[(m + 1) % 2], q_made)

                def project_k(n, m):
                    if m < 2:
                        pe.wait_ge(q_kept, CHUNKS * n + m + 2)
                    else:
                        pe.wait_ge(k_kept_act, CHUNKS * n + 1)
                        pe.wait_ge(k_kept_dve, CHUNKS * n + 1)
                    project_chunk(n, WK, m, proj_bank[m % 2], k_made)

                def project_v(n, b):
                    if b >= 2:
                        pe.wait_ge(v_kept, GROUP * n + b - 1)
                    for c in range(CHUNKS):
                        mm = product(proj_bank[b % 2][:, 0:FEATURES], hT_high[:, c, b], hT_low[:, c, b],
                                     weights_high[:, WV, c], weights_low[:, WV, c], c)
                    mm.then_inc(v_made, 1)

                def scores(n, b, m):
                    if b == 0:
                        pe.wait_ge(q_kept, CHUNKS * n + m + 1)
                        pe.wait_ge(k_kept_act, CHUNKS * n + m + 1)
                        pe.wait_ge(k_kept_dve, CHUNKS * n + m + 1)
                    t = CHUNKS * b + m
                    pe.wait_ge(scores_kept, BANKS_PER_GROUP * n + max(t - 1, 0))
                    pe.matmul(score_bank[t % 2][:, :], qT[:, m, b], kT[:, m, b], start=True, stop=True
                              ).then_inc(scores_made, 1)

                def transpose_probs(n, b, m):
                    t = CHUNKS * b + m
                    if m == 0:
                        pe.wait_ge(probs_ready, GROUP * n + b + 1)
                    pe.wait_ge(probsT_kept, BANKS_PER_GROUP * n + max(t - 1, 0))
                    for g in range(PER_CHUNK):
                        mm = pe.transpose(probsT_bank[t % 2][:, g * 128:(g + 1) * 128],
                                          probs[:, b, m * PER_CHUNK + g], ident)
                    mm.then_inc(probsT_made, 1)

                def weigh_values(n, b, m):
                    if m == 0:
                        pe.wait_ge(v_kept, GROUP * n + b + 1)
                        pe.wait_ge(headsT_kept, GROUP * n + b)
                    pe.wait_ge(probsT_kept, BANKS_PER_GROUP * n + CHUNKS * b + m + 1)
                    row = values[:, b].rearrange("p h w -> p (h w)")
                    for g in range(PER_CHUNK):
                        at = (m * PER_CHUNK + g) * 128 - g * HEAD
                        mm = pe.matmul(headsT_bank[:, m * 128:(m + 1) * 128], row[:, at:at + 128], probsT[:, m, g],
                                       start=g == 0, stop=g == PER_CHUNK - 1)
                    if m == CHUNKS - 1:
                        mm.then_inc(headsT_made, 1)

                def attend_and_project(n, b, with_scores=False):
                    transpose_probs(n, b, 0)
                    transpose_probs(n, b, 1)
                    if with_scores:
                        scores(n + 1, 1, 2)
                    weigh_values(n, b, 0)
                    transpose_probs(n, b, 2)
                    project_out(n, b - 1)
                    weigh_values(n, b, 1)
                    weigh_values(n, b, 2)

                def project_out(n, b):
                    pe.wait_ge(headsT_kept, GROUP * n + b + 1)
                    pe.wait_ge(a_y_kept, GROUP * n + b)
                    for c in range(CHUNKS):
                        mm = product(y_bank[:, 0:FEATURES], headsT_high[:, b % 2, c], headsT_low[:, b % 2, c],
                                     weights_high[:, WO, c], weights_low[:, WO, c], c)
                    mm.then_inc(y_made, 1)

                def body(n, i, first, last):
                    scores(n, 0, 0)
                    scores(n, 0, 1)
                    if not first:
                        transpose_probs(n - 1, 2, 0)
                        transpose_probs(n - 1, 2, 1)
                    scores(n, 0, 2)
                    if first:
                        pe.wait_ge(weights_split, splits_of_weight(p, WV))
                    project_v(n, 0)
                    if not first:
                        weigh_values(n - 1, 2, 0)
                        transpose_probs(n - 1, 2, 2)
                    project_v(n, 1)
                    if not first:
                        weigh_values(n - 1, 2, 1)
                        weigh_values(n - 1, 2, 2)
                    scores(n, 1, 0)
                    scores(n, 1, 1)
                    if not first:
                        attend_and_project(n - 1, 3, with_scores=True)
                    else:
                        scores(n, 1, 2)
                    scores(n, 2, 0)
                    project_v(n, 2)
                    scores(n, 2, 1)
                    project_v(n, 3)
                    if not first:
                        project_out(n - 1, 3)
                    scores(n, 2, 2)
                    transpose_probs(n, 0, 0)
                    transpose_probs(n, 0, 1)
                    scores(n, 3, 0)
                    weigh_values(n, 0, 0)
                    transpose_probs(n, 0, 2)
                    scores(n, 3, 1)
                    weigh_values(n, 0, 1)
                    weigh_values(n, 0, 2)
                    transpose_probs(n, 1, 0)
                    transpose_probs(n, 1, 1)
                    scores(n, 3, 2)
                    weigh_values(n, 1, 0)
                    transpose_probs(n, 1, 2)
                    weigh_values(n, 1, 1)
                    if not last:
                        transpose_h(n + 1, 0, False)
                        transpose_h(n + 1, 1, False)
                    if first:
                        pe.wait_ge(weights_split, splits_of_weight(p, WO))
                    project_out(n, 0)
                    weigh_values(n, 1, 2)
                    if not last:
                        transpose_h(n + 1, 2, False)
                        project_q(n + 1, 0)
                        project_out(n, 1)
                        project_q(n + 1, 1)
                        project_q(n + 1, 2)
                        for m in range(CHUNKS):
                            project_k(n + 1, m)
                    else:
                        transpose_probs(n, 2, 0)
                        transpose_probs(n, 2, 1)
                        weigh_values(n, 2, 0)
                        transpose_probs(n, 2, 2)
                        project_out(n, 1)
                        weigh_values(n, 2, 1)
                        weigh_values(n, 2, 2)
                        attend_and_project(n, 3)
                        project_out(n, 3)

                n0 = first_group(p)
                for c in range(CHUNKS):
                    transpose_h(n0, c, True)
                pe.wait_ge(weights_split, splits_of_weight(p, WQ))
                for m in range(CHUNKS):
                    project_q(n0, m)
                pe.wait_ge(weights_split, splits_of_weight(p, WK))
                for m in range(CHUNKS):
                    project_k(n0, m)
                groups_of(pe, p, body)

            def convolution(p):
                WL, WR, WS = range(3)

                def project(n, b, w, to, kept, made, first):
                    if first and b == 0:
                        pe.wait_ge(weights_split, splits_of_weight(p, w))
                    pe.wait_ge(gT_split, GROUP * n + b + 1)
                    pe.wait_ge(kept, GROUP * n + b)
                    for c in range(CHUNKS):
                        mm = product(to[:, 0:FEATURES], gT_high[:, b % 2, c], gT_low[:, b % 2, c],
                                     weights_high[:, w, c], weights_low[:, w, c], c)
                    mm.then_inc(made, 1)

                def transpose_attn(n, b):
                    pe.wait_ge(attn_done, GROUP * n + b + 1)
                    pe.wait_ge(attnT_kept, GROUP * n + b)
                    pe.transpose(attnT_bank[:, 0:128], attn[:], ident).then_inc(attnT_made, 1)

                def transpose_g(of, n, b):
                    if normalises(of):
                        pe.wait_ge(h_made, GROUP * normalised(of, n) + b + 1)
                    else:
                        pe.wait_ge(c_h_loaded[b], 16 * (n - first_group(of)) + 16)
                    pe.wait_ge(gT_rounded, GROUP * n + b)
                    for c in range(CHUNKS):
                        mm = pe.transpose(gT_bank[:, c * 128:(c + 1) * 128], hs[:, b, c * 128:(c + 1) * 128], ident)
                    mm.then_inc(gT_made, 1)

                def gram(n, b):
                    pe.wait_ge(gT_kept, GROUP * n + b + 1)
                    pe.wait_ge(u_exp_done, GROUP * n + b)
                    for c in range(CHUNKS):
                        mm = pe.matmul(u_bank[:, 0:128], gT[:, b % 2, c], gT[:, b % 2, c],
                                       start=c == 0, stop=c == CHUNKS - 1)
                    mm.then_inc(u_made, 1)

                def mix(n, b):
                    pe.wait_ge(mix_kept, GROUP * n + b)
                    pe.wait_ge(attnT_kept, GROUP * n + b + 1)
                    pe.wait_ge(left_kept, GROUP * n + b + 1)
                    pe.matmul(mix_bank[:, 0:FEATURES], attn_leftT[:], left[:], start=True, stop=False)
                    pe.wait_ge(right_kept, GROUP * n + b + 1)
                    pe.matmul(mix_bank[:, 0:FEATURES], attn_rightT[:], right[:], start=False, stop=True
                              ).then_inc(mix_made, 1)

                def body(n, i, first, last):
                    for b in range(GROUP):
                        more, n1, b1, of = after(p, n, b, last)
                        project(n, b, WL, left_bank, left_kept, left_made, first)
                        transpose_attn(n, b)
                        if more:
                            transpose_g(of, n1, b1)
                        project(n, b, WR, right_bank, right_kept, right_made, first)
                        if more:
                            gram(n1, b1)
                        project(n, b, WS, own_bank, own_copied, own_made, first)
                        mix(n, b)

                n0 = first_group(p)
                if not goes_on(p - 1):
                    transpose_g(p, n0, 0)
                    gram(n0, 0)
                groups_of(pe, p, body)

            pe.wait_ge(consts_loaded, 16)
            for p in range(len(PASSES)):
                (attention if is_attention(p) else convolution)(p)
                finish_pass(pe, p)

        @block.scalar
        def _(act):
            def normalise(number, b):
                if b == 0:
                    act.wait_ge(rstd_done, number + 1)
                act.activation(hs[:, b], xs[:, b], ACT.Relu, bias=shift[:, b:b + 1],
                               scale=rstd[:, b:b + 1]).then_inc(h_made, 1)

            def normalise_out(count, b):
                act.wait_ge(o_rstd_done, count)
                act.activation(normed[:], mixed[:, b % 2], ACT.Identity, bias=o_shift[:, b % 2:b % 2 + 1],
                               scale=o_rstd[:, b % 2:b % 2 + 1]).then_inc(o_normed, 1)

            def round_weight(p, w):
                act.wait_ge(weight_loaded[w], loads_of_weight(p, w))
                act.copy(flat(weights_high[:, w]), flat(weights[:, w])).then_inc(weights_rounded, 1)

            def attention(p):
                def round_hT(n, c):
                    act.wait_ge(hT_made, CHUNKS * n + c + 1)
                    act.copy(flat(hT_high[:, c]), proj_bank[c % 2][:, :]).then_inc(hT_rounded, 1)

                def keep_q(n, m):
                    act.wait_ge(q_made, CHUNKS * n + m + 1)
                    act.mul(flat(qT[:, m]), proj_bank[(m + 1) % 2][:, :], SCALE).then_inc(q_kept, 1)

                def keep_k(n, m):
                    act.wait_ge(k_made, CHUNKS * n + m + 1)
                    for g in (0, 1):
                        ins = act.copy(kT[g * HEAD:(g + 1) * HEAD, m, :, g],
                                       proj_bank[m % 2][g * HEAD:(g + 1) * HEAD, :].rearrange("p (b n) -> p b n", b=GROUP))
                    ins.then_inc(k_kept_act, 1)

                def exponentials(n, b):
                    act.wait_ge(max_taken, GROUP * n + b + 1)
                    act.activation(probs[:, b], probs[:, b], ACT.Exp).then_inc(exp_done, 1)

                def keep_probsT(n, b, m):
                    t = CHUNKS * b + m
                    act.wait_ge(probsT_made, BANKS_PER_GROUP * n + t + 1)
                    act.copy(flat(probsT[:, m]), probsT_bank[t % 2][:, :]).then_inc(probsT_kept, 1)

                def round_headsT(n, b):
                    act.wait_ge(headsT_made, GROUP * n + b + 1)
                    act.copy(flat(headsT_high[:, b % 2]), headsT_bank[:, 0:FEATURES]).then_inc(headsT_rounded, 1)

                def hold_x(n):
                    act.wait_ge(x_loaded, 16 * normalised(p, n) + 16)
                    act.wait_ge(res_made, GROUP * n + 2)
                    for b in (2, 3):
                        act.copy(held_x[:, b - 2], xs[:, b]).then_inc(x_held, 1)

                def keep_all_probsT(n, b):
                    for m in range(CHUNKS):
                        keep_probsT(n, b, m)

                def body(n, i, first, last):
                    following = next_normalised(p, n, last)
                    if not first:
                        keep_all_probsT(n - 1, 2)
                    hold_x(n)
                    if not first:
                        round_headsT(n - 1, 2)
                    if not first:
                        keep_probsT(n - 1, 3, 0)
                        keep_probsT(n - 1, 3, 1)
                    exponentials(n, 0)
                    if not first:
                        keep_probsT(n - 1, 3, 2)
                    if not first:
                        round_headsT(n - 1, 3)
                    exponentials(n, 1)
                    keep_all_probsT(n, 0)
                    if not last and following is not None:
                        normalise(following, 0)
                    round_headsT(n, 0)
                    keep_probsT(n, 1, 0)
                    keep_probsT(n, 1, 1)
                    if not last and following is not None:
                        for b in (1, 2, 3):
                            normalise(following, b)
                    keep_probsT(n, 1, 2)
                    if not last:
                        for c in range(CHUNKS):
                            round_hT(n + 1, c)
                        round_headsT(n, 1)
                        keep_q(n + 1, 0)
                        exponentials(n, 2)
                        keep_q(n + 1, 1)
                        keep_q(n + 1, 2)
                        exponentials(n, 3)
                        keep_k(n + 1, 0)
                        keep_k(n + 1, 1)
                        keep_k(n + 1, 2)
                    else:
                        exponentials(n, 2)
                        round_headsT(n, 1)
                        exponentials(n, 3)
                        keep_all_probsT(n, 2)
                        if following is not None:
                            for b in range(GROUP):
                                normalise(following, b)
                        round_headsT(n, 2)
                        keep_all_probsT(n, 3)
                        round_headsT(n, 3)

                n0 = first_group(p)
                if not meets_attention(p - 1):
                    round_weight(p, 0)
                for c in range(CHUNKS):
                    round_hT(n0, c)
                if not meets_attention(p - 1):
                    round_weight(p, 1)
                else:
                    round_weight(p, 2)
                    round_weight(p, 3)
                    normalise_out(GROUP * (first_group(p - 1) + GROUPS), GROUP - 1)
                for m in range(CHUNKS):
                    keep_q(n0, m)
                    if m < 2 and not meets_attention(p - 1):
                        round_weight(p, 2 + m)
                if p == 0:
                    act.wait_ge(keys_zeroed, 1)
                for m in range(CHUNKS):
                    keep_k(n0, m)
                groups_of(act, p, body)

            def convolution(p):
                def keep_gT(n, b):
                    act.wait_ge(gT_made, GROUP * n + b + 1)
                    act.copy(flat(gT[:, b % 2]), gT_bank[:, 0:FEATURES]).then_inc(gT_kept, 1)
                    act.copy(flat(gT_high[:, b % 2]), gT_bank[:, 0:FEATURES]).then_inc(gT_rounded, 1)

                def copy_own(n, b):
                    act.wait_ge(own_made, GROUP * n + b + 1)
                    act.wait_ge(mix_kept, GROUP * n + b)
                    act.copy(own[:], own_bank[:, 0:FEATURES]).then_inc(own_copied, 1)

                def exponentials(n, b):
                    act.wait_ge(u_max_found, GROUP * n + b + 1)
                    act.mul(neg_max_scaled[:], neg_max[:], SCALE).then_inc(u_max_scaled, 1)
                    act.wait_ge(u_max_scaled, GROUP * n + b + 1)
                    act.activation(e[:], u_bank[:, 0:128], ACT.Exp, bias=neg_max_scaled[:], scale=SCALE,
                                   accum_out=e_sum[:]).then_inc(u_exp_done, 1)

                def body(n, i, first, last):
                    following = next_normalised(p, n, last)
                    for b in range(GROUP):
                        more, n1, b1, of = after(p, n, b, last)
                        another, b_before, _ = before(p, b, first)
                        if more:
                            keep_gT(n1, b1)
                        ends = last and b == GROUP - 1
                        if ends:
                            act.wait_ge(left_made, GROUP * n1)
                            round_weight(p + 1, 0)
                        if another:
                            normalise_out(GROUP * n + b, b_before)
                        if more:
                            exponentials(n1, b1)
                        if ends:
                            act.wait_ge(right_made, GROUP * n1)
                            round_weight(p + 1, 1)
                        copy_own(n, b)
                        if ends and goes_on(p):
                            act.wait_ge(own_made, GROUP * n1)
                            round_weight(p + 1, 2)
                        if b == 2 and following is not None:
                            for b2 in range(GROUP):
                                normalise(following, b2)

                n0 = first_group(p)
                if not goes_on(p - 1):
                    round_weight(p, 0)
                    keep_gT(n0, 0)
                    round_weight(p, 1)
                    exponentials(n0, 0)
                    round_weight(p, 2)
                groups_of(act, p, body)

            for b in range(GROUP):
                normalise(0, b)
            for p in range(len(PASSES)):
                (attention if is_attention(p) else convolution)(p)
                finish_pass(act, p)

        @block.gpsimd
        def _(pool):
            def reciprocal_deviation(n):
                pool.wait_ge(var_done, n + 1)
                pool.tensor_tensor(rstd[:], var_eps[:], minus_half[:], ALU.pow).then_inc(pow_done, 1)
                pool.wait_ge(pow_done, n + 1)
                pool.tensor_tensor(shift[:], neg_mean[:], rstd[:], ALU.mult).then_inc(rstd_done, 1)

            def attention(p):
                BV, BO = range(2)
                pool.wait_ge(vectors_loaded[p], 16 * len(vectors_in[p]))

                def keep_residual(n, b, first):
                    if first and meets_attention(p - 1):
                        pool.wait_ge(c_y_kept, GROUP * (first_group(p - 1) + GROUPS))
                    if not first:
                        pool.wait_ge(a_y_kept, GROUP * (n - 1) + b + 1)
                    if b < 2:
                        pool.wait_ge(x_loaded, 16 * normalised(p, n) + 16)
                        x_of = xs[:, b]
                    else:
                        pool.wait_ge(x_held, 2 * n + b - 1)
                        x_of = held_x[:, b - 2]
                    pool.tensor_tensor(res[:, b], x_of, vector(p, BO), ALU.add).then_inc(res_made, 1)

                def take_max(n, b):
                    pool.wait_ge(abs_found, GROUP * n + b + 1)
                    pool.tensor_tensor(probs[:, b], probs[:, b],
                                       row_max[:, b].unsqueeze(2).to_broadcast([128, HEADS, NODES]),
                                       ALU.subtract).then_inc(max_taken, 1)

                def normalise_probs(n, b):
                    pool.wait_ge(sums_guarded, GROUP * n + b + 1)
                    pool.tensor_tensor(probs[:, b], probs[:, b],
                                       inv_kept[:, b].unsqueeze(2).to_broadcast([128, HEADS, NODES]),
                                       ALU.mult).then_inc(probs_ready, 1)

                def body(n, i, first, last):
                    for b in (0, 1):
                        keep_residual(n, b, first)
                    if not first:
                        normalise_probs(n - 1, 3)
                    take_max(n, 0)
                    take_max(n, 1)
                    normalise_probs(n, 0)
                    normalise_probs(n, 1)
                    following = next_normalised(p, n, last)
                    if not last and following is not None:
                        reciprocal_deviation(following)
                    for b in (2, 3):
                        keep_residual(n, b, first)
                    take_max(n, 2)
                    take_max(n, 3)
                    normalise_probs(n, 2)
                    if last:
                        if following is not None:
                            reciprocal_deviation(following)
                        normalise_probs(n, 3)

                groups_of(pool, p, body)

            def convolution(p):
                BL, BR, BS, GAMMA, BETA = range(5)

                def add_own_bias(n, b):
                    pool.wait_ge(own_copied, GROUP * n + b + 1)
                    pool.tensor_tensor(own[:], own[:], vector(p, BS), ALU.add).then_inc(own_kept, 1)

                def split_gT(n, b):
                    pool.wait_ge(gT_rounded, GROUP * n + b + 1)
                    pool.tensor_tensor(flat(gT_low[:, b % 2]), flat(gT[:, b % 2]), flat(gT_high[:, b % 2]).bitcast(F32),
                                       ALU.subtract).then_inc(gT_split, 1)

                def out_deviation(count, b):
                    pool.wait_ge(o_var, count)
                    pool.tensor_tensor(o_rstd[:, b % 2:b % 2 + 1], o_var_eps[:], minus_half[:, 0:1], ALU.pow
                                       ).then_inc(o_pow, 1)
                    pool.wait_ge(o_pow, count)
                    pool.tensor_tensor(o_shift[:, b % 2:b % 2 + 1], o_neg_mean[:], o_rstd[:, b % 2:b % 2 + 1],
                                       ALU.mult).then_inc(o_rstd_done, 1)

                def scale_and_shift(of, count):
                    pool.wait_ge(o_normed, count)
                    pool.tensor_tensor(normed[:], normed[:], vector(of, GAMMA), ALU.mult).then_inc(o_scaled, 1)
                    pool.wait_ge(o_scaled, count)
                    pool.tensor_tensor(normed[:], normed[:], vector(of, BETA), ALU.add).then_inc(o_shifted, 1)

                def body(n, i, first, last):
                    following = next_normalised(p, n, last)
                    for b in range(GROUP):
                        more, n1, b1, _ = after(p, n, b, last)
                        another, b_before, of = before(p, b, first)
                        if another:
                            out_deviation(GROUP * n + b, b_before)
                        if more:
                            split_gT(n1, b1)
                        if another:
                            scale_and_shift(of, GROUP * n + b)
                        add_own_bias(n, b)
                        if b == 1 and following is not None:
                            reciprocal_deviation(following)
                    if last and not goes_on(p):
                        out_deviation(GROUP * n + GROUP, GROUP - 1)
                        scale_and_shift(p, GROUP * n + GROUP)

                if not goes_on(p - 1):
                    split_gT(first_group(p), 0)
                pool.wait_ge(vectors_loaded[p], 16 * len(vectors_in[p]))
                groups_of(pool, p, body)

            pool.memset(minus_half[:], -0.5)
            pool.memset(kT[:], 0.0).then_inc(keys_zeroed, 1)
            pool.wait_ge(keys_zeroed, 1)
            reciprocal_deviation(0)
            pool.memset(values[:], 0.0).then_inc(values_zeroed, 1)
            for p in range(len(PASSES)):
                (attention if is_attention(p) else convolution)(p)
                finish_pass(pool, p)

        @block.vector
        def _(dve):
            def wait_in_memset(sem_, value):
                dve.wait_ge(sem_, value)
                dve.memset(spare[:], 0.0)

            def split_weight(p, w):
                dve.wait_ge(weight_loaded[w], loads_of_weight(p, w))
                dve.wait_ge(weights_rounded, splits_of_weight(p, w))
                dve.tensor_tensor(flat(weights_low[:, w]), flat(weights[:, w]), flat(weights_high[:, w]).bitcast(F32),
                                  ALU.subtract).then_inc(weights_split, 1)

            def wait_stored_before(p, b):
                if is_attention(p) and p > 0:
                    dve.wait_ge(c_y_stored[b], 16 * (first_group(p - 1) + GROUPS))
                elif not is_attention(p) and is_attention(p - 1):
                    dve.wait_ge(a_y_stored[b // 2], 16 * (first_group(p - 1) + GROUPS))

            def residual_of(of, n):
                with_one = sum(1 for q in range(of) if not is_attention(q) and residual[q] is not None)
                return 16 * (n - first_group(of) + GROUPS * with_one) + 16

            def keep_convolved_y(of, n, b, count):
                dve.wait_ge(c_y_stored[b], 16 * n)
                if residual[of] is not None:
                    dve.wait_ge(c_res_loaded[b], residual_of(of, n))
                dve.wait_ge(o_shifted, count)
                if residual[of] is not None:
                    dve.scalar_tensor_tensor(out=ys[:, b], in0=normed[:], scalar=0.0, in1=res[:, b],
                                             op0=ALU.max, op1=ALU.add).then_inc(c_y_kept, 1)
                else:
                    dve.tensor_scalar(ys[:, b], normed[:], 0.0, None, ALU.max).then_inc(c_y_kept, 1)

            def split_hT(n, c):
                dve.wait_ge(hT_rounded, CHUNKS * n + c + 1)
                dve.tensor_tensor(flat(hT_low[:, c]), proj_bank[c % 2][:, :], flat(hT_high[:, c]).bitcast(F32),
                                  ALU.subtract).then_inc(hT_kept, 1)

            def moments_of(n):
                dve.wait_ge(x_loaded, 16 * n + 16)
                for b in range(GROUP):
                    ins = dve.bn_stats(stats[:, b], xs[:, b])
                ins.then_inc(bn_done, 1)
                wait_in_memset(bn_done, n + 1)
                for b in range(GROUP):
                    ins = dve.bn_aggr(moments[:, b], stats[:, b])
                ins.then_inc(mv_done, 1)
                dve.wait_ge(mv_done, n + 1)
                dve.tensor_scalar(neg_mean[:], moments[:, :, 0], -1.0, None, ALU.mult)
                dve.tensor_scalar(var_eps[:], moments[:, :, 1], EPS_IN, None, ALU.add).then_inc(var_done, 1)

            def attention(p):
                BV, BO = range(2)
                n0 = first_group(p)

                def keep_k(n, m):
                    dve.wait_ge(k_made, CHUNKS * n + m + 1)
                    for g in (2, 3):
                        ins = dve.tensor_copy(kT[g * HEAD:(g + 1) * HEAD, m, :, g],
                                              proj_bank[m % 2][g * HEAD:(g + 1) * HEAD, :]
                                              .rearrange("p (b n) -> p b n", b=GROUP))
                    ins.then_inc(k_kept_dve, 1)

                def split_headsT(n, b):
                    dve.wait_ge(headsT_rounded, GROUP * n + b + 1)
                    dve.tensor_tensor(flat(headsT_low[:, b % 2]), headsT_bank[:, 0:FEATURES],
                                      flat(headsT_high[:, b % 2]).bitcast(F32), ALU.subtract).then_inc(headsT_kept, 1)

                def keep_v(n, b):
                    dve.wait_ge(v_made, GROUP * n + b + 1)
                    dve.tensor_tensor(values[:, b, :, 0:HEAD],
                                      proj_bank[b % 2][:, 0:FEATURES].rearrange("p (h w) -> p h w", w=HEAD),
                                      vector(p, BV).rearrange("p (h w) -> p h w", w=HEAD), ALU.add).then_inc(v_kept, 1)

                def add_bias(n, b, m):
                    if b == 0 and m == 0:
                        dve.wait_ge(a_adj_loaded, 16 * n + 16)
                    t = CHUNKS * b + m
                    dve.wait_ge(scores_made, BANKS_PER_GROUP * n + t + 1)
                    dve.scalar_tensor_tensor(
                        out=probs[:, b, m * PER_CHUNK:(m + 1) * PER_CHUNK],
                        in0=adj[:, b].unsqueeze(1).to_broadcast([128, PER_CHUNK, NODES]),
                        scalar=BIAS_TIMES[PASSES[p]],
                        in1=score_bank[t % 2][:, :].rearrange("p (g n) -> p g n", g=PER_CHUNK),
                        op0=ALU.mult, op1=ALU.add).then_inc(scores_kept, 1)

                def find_max(n, b):
                    dve.wait_ge(scores_kept, BANKS_PER_GROUP * n + CHUNKS * b + CHUNKS)
                    dve.tensor_reduce(row_max[:, b], probs[:, b], AX.X, ALU.max).then_inc(max_found, 1)

                def find_abs(n, b):
                    dve.tensor_reduce(row_abs[:, b], probs[:, b], AX.X, ALU.max, apply_absolute_value=True
                                      ).then_inc(abs_found, 1)

                def invert_sums(n, b):
                    dve.wait_ge(exp_done, GROUP * n + b + 1)
                    dve.tensor_reduce(row_sum[:, b], probs[:, b], AX.X, ALU.add).then_inc(sums_found, 1)
                    dve.wait_ge(sums_found, GROUP * n + b + 1)
                    dve.reciprocal(inv_sum[:, b], row_sum[:, b]).then_inc(sums_inverted, 1)
                    dve.wait_ge(sums_inverted, GROUP * n + b + 1)
                    dve.scalar_tensor_tensor(out=inv_kept[:, b], in0=row_abs[:, b], scalar=0.0, in1=inv_sum[:, b],
                                             op0=ALU.is_gt, op1=ALU.mult).then_inc(sums_guarded, 1)

                def keep_y(n, b):
                    dve.wait_ge(a_y_stored[b // 2], 16 * n)
                    dve.wait_ge(res_made, GROUP * n + b + 1)
                    dve.wait_ge(y_made, GROUP * n + b + 1)
                    dve.tensor_tensor(ys[:, b], y_bank[:, 0:FEATURES], res[:, b], ALU.add).then_inc(a_y_kept, 1)

                def body(n, i, first, last):
                    for m in range(CHUNKS):
                        add_bias(n, 0, m)
                    if not first:
                        invert_sums(n - 1, 3)
                    keep_v(n, 0)
                    find_max(n, 0)
                    find_abs(n, 0)
                    keep_v(n, 1)
                    if not first:
                        split_headsT(n - 1, 2)
                    for m in range(CHUNKS):
                        add_bias(n, 1, m)
                    find_max(n, 1)
                    find_abs(n, 1)
                    invert_sums(n, 0)
                    if not first:
                        keep_y(n - 1, 2)
                        split_headsT(n - 1, 3)
                    add_bias(n, 2, 0)
                    keep_v(n, 2)
                    add_bias(n, 2, 1)
                    keep_v(n, 3)
                    invert_sums(n, 1)
                    add_bias(n, 2, 2)
                    if not first:
                        keep_y(n - 1, 3)
                    following = next_normalised(p, n, last)
                    if not last:
                        moments_of(following)
                        add_bias(n, 3, 0)
                        split_headsT(n, 0)
                        add_bias(n, 3, 1)
                        find_max(n, 2)
                        add_bias(n, 3, 2)
                        find_abs(n, 2)
                    else:
                        find_max(n, 2)
                        add_bias(n, 3, 0)
                        find_abs(n, 2)
                        split_headsT(n, 0)
                        add_bias(n, 3, 1)
                        add_bias(n, 3, 2)
                    if not last:
                        split_hT(n + 1, 0)
                        split_hT(n + 1, 1)
                        keep_y(n, 0)
                        split_hT(n + 1, 2)
                        split_headsT(n, 1)
                        find_max(n, 3)
                        find_abs(n, 3)
                        keep_y(n, 1)
                        invert_sums(n, 2)
                        for m in range(CHUNKS):
                            keep_k(n + 1, m)
                    else:
                        find_max(n, 3)
                        find_abs(n, 3)
                        invert_sums(n, 2)
                        keep_y(n, 0)
                        split_headsT(n, 1)
                        if following is not None:
                            moments_of(following)
                        invert_sums(n, 3)
                        keep_y(n, 1)
                        split_headsT(n, 2)
                        keep_y(n, 2)
                        split_headsT(n, 3)
                        keep_y(n, 3)

                if meets_attention(p - 1):
                    split_hT(n0, 2)
                else:
                    split_weight(p, 0)
                    for c in range(CHUNKS):
                        split_hT(n0, c)
                    split_weight(p, 1)
                split_weight(p, 2)
                split_weight(p, 3)
                if meets_attention(p - 1):
                    last_n = first_group(p - 1) + GROUPS - 1
                    keep_convolved_y(p - 1, last_n, GROUP - 1, GROUP * last_n + GROUP)
                dve.wait_ge(vectors_loaded[p], 16 * len(vectors_in[p]))
                if p == 0:
                    dve.wait_ge(keys_zeroed, 1)
                    dve.wait_ge(values_zeroed, 1)
                for b in range(GROUP):
                    wait_stored_before(p, b)
                for m in range(CHUNKS):
                    keep_k(n0, m)
                groups_of(dve, p, body)

            def convolution(p):
                BL, BR, BS, GAMMA, BETA = range(5)
                n0 = first_group(p)

                def keep_side(n, b, to, bank_, v, made, kept):
                    dve.wait_ge(made, GROUP * n + b + 1)
                    dve.tensor_tensor(to[:], bank_[:, 0:FEATURES], vector(p, v), ALU.add).then_inc(kept, 1)

                def split_attn(n, b):
                    dve.wait_ge(attnT_made, GROUP * n + b + 1)
                    dve.tensor_tensor(attn_leftT[:], attnT_bank[:, 0:128], later, ALU.mult)
                    dve.tensor_tensor(attn_rightT[:], attnT_bank[:, 0:128], earlier, ALU.mult).then_inc(attnT_kept, 1)

                def find_max(n, b):
                    dve.wait_ge(u_made, GROUP * n + b + 1)
                    dve.tensor_reduce(neg_max[:], u_bank[:, 0:128], AX.X, ALU.max, negate=True).then_inc(u_max_found, 1)

                def attention_rows(n, b):
                    dve.wait_ge(c_adj_loaded[b], 16 * n + 16)
                    dve.wait_ge(u_exp_done, GROUP * n + b + 1)
                    dve.tensor_tensor_reduce(out=e_adj[:], in0=e[:], in1=adj[:, b], scale=1.0, scalar=0.0,
                                             op0=ALU.mult, op1=ALU.add, accum_out=e_adj_sum[:]).then_inc(e_adj_done, 1)
                    dve.wait_ge(e_adj_done, GROUP * n + b + 1)
                    dve.scalar_tensor_tensor(out=denom[:], in0=e_sum[:], scalar=EPS_SUM, in1=e_adj_sum[:],
                                             op0=ALU.mult, op1=ALU.add).then_inc(denom_done, 1)
                    dve.wait_ge(denom_done, GROUP * n + b + 1)
                    dve.reciprocal(inv_denom[:], denom[:]).then_inc(denom_inverted, 1)
                    dve.wait_ge(denom_inverted, GROUP * n + b + 1)
                    dve.tensor_scalar(attn[:], e_adj[:], inv_denom[:], None, ALU.mult).then_inc(attn_done, 1)
                    dve.wait_ge(attn_done, GROUP * n + b + 1)
                    dve.tensor_tensor_reduce(out=attn_ident[:], in0=attn[:], in1=ident, scale=1.0, scalar=0.0,
                                             op0=ALU.mult, op1=ALU.add, accum_out=diag[:, b % 2:b % 2 + 1]
                                             ).then_inc(diag_done, 1)

                def mix_own(n, b):
                    dve.wait_ge(own_kept, GROUP * n + b + 1)
                    dve.wait_ge(diag_done, GROUP * n + b + 1)
                    dve.wait_ge(mix_made, GROUP * n + b + 1)
                    dve.scalar_tensor_tensor(out=mixed[:, b % 2], in0=own[:], scalar=diag[:, b % 2:b % 2 + 1],
                                             in1=mix_bank[:, 0:FEATURES], op0=ALU.mult, op1=ALU.add
                                             ).then_inc(mix_kept, 1)
                    dve.wait_ge(mix_kept, GROUP * n + b + 1)
                    dve.bn_stats(o_stats[:], mixed[:, b % 2]).then_inc(o_bn, 1)
                    wait_in_memset(o_bn, GROUP * n + b + 1)
                    dve.bn_aggr(o_moments[:], o_stats[:]).then_inc(o_mv, 1)
                    dve.wait_ge(o_mv, GROUP * n + b + 1)
                    dve.tensor_scalar(o_neg_mean[:], o_moments[:, 0:1], -1.0, None, ALU.mult)
                    dve.tensor_scalar(o_var_eps[:], o_moments[:, 1:2], EPS_OUT, None, ALU.add).then_inc(o_var, 1)

                def body(n, i, first, last):
                    following = next_normalised(p, n, last)
                    for b in range(GROUP):
                        more, n1, b1, of = after(p, n, b, last)
                        another, b_before, of_before = before(p, b, first)
                        keep_side(n, b, left, left_bank, BL, left_made, left_kept)
                        split_attn(n, b)
                        keep_side(n, b, right, right_bank, BR, right_made, right_kept)
                        if b == 1 and following is not None:
                            moments_of(following)
                        if more:
                            find_max(n1, b1)
                        ends = last and b == GROUP - 1
                        if ends:
                            split_weight(p + 1, 0)
                        if more:
                            attention_rows(n1, b1)
                        if ends:
                            split_weight(p + 1, 1)
                            if meets_attention(p):
                                split_hT(first_group(p + 1), 0)
                                split_hT(first_group(p + 1), 1)
                        if another:
                            keep_convolved_y(of_before, n if b > 0 else n - 1, b_before, GROUP * n + b)
                        mix_own(n, b)
                        if ends and goes_on(p):
                            split_weight(p + 1, 2)

                if not goes_on(p - 1):
                    split_weight(p, 0)
                    find_max(n0, 0)
                    split_weight(p, 1)
                    split_weight(p, 2)
                    attention_rows(n0, 0)
                dve.wait_ge(vectors_loaded[p], 16 * len(vectors_in[p]))
                for b in range(GROUP):
                    wait_stored_before(p, b)
                groups_of(dve, p, body)

            dve.wait_ge(consts_loaded, 16)
            moments_of(0)
            for p in range(len(PASSES)):
                (attention if is_attention(p) else convolution)(p)
                finish_pass(dve, p)


def kernel(x, adj, L0_gnn_Wq, L0_gnn_Wk, L0_gnn_Wv, L0_gnn_bv, L0_gnn_Wo, L0_gnn_bo, L1_gnn_W_left, L1_gnn_b_left,
           L1_gnn_W_self, L1_gnn_b_self, L1_gnn_W_right, L1_gnn_b_right, L1_gnn_gamma, L1_gnn_beta, L2_gnn_Wl,
           L2_gnn_bl, L2_gnn_Ws, L2_gnn_bs, L2_gnn_Wr, L2_gnn_br, L2_gnn_ln_w, L2_gnn_ln_b, L3_gnn_Wq, L3_gnn_Wk,
           L3_gnn_Wv, L3_gnn_bv, L3_gnn_Wo, L3_gnn_bo):
    import numpy as np
    import concourse.bacc as bacc
    from concourse.bass_utils import run_bass_kernel_spmd

    nc = bacc.Bacc("TRN2", target_bir_lowering=False, num_devices=1)
    arrays = {}

    def give(name, a):
        arrays[name] = np.ascontiguousarray(a)
        return nc.dram_tensor(name, arrays[name].shape, mybir.dt.from_np(arrays[name].dtype),
                              kind="ExternalInput").ap()

    row, column = np.indices((128, 128))
    consts = np.stack([row == column, row > column, row < column], axis=1).astype(np.float32)
    weights = (
        (L0_gnn_Wq, L0_gnn_Wk, L0_gnn_Wv, L0_gnn_Wo),
        (L1_gnn_W_left, L1_gnn_W_right, L1_gnn_W_self),
        (L2_gnn_Wl[0], L2_gnn_Wr[0], L2_gnn_Ws[0]),
        (L2_gnn_Wl[1], L2_gnn_Wr[1], L2_gnn_Ws[1]),
        (L3_gnn_Wq, L3_gnn_Wk, L3_gnn_Wv, L3_gnn_Wo),
    )
    vectors = (
        (L0_gnn_bv, L0_gnn_bo),
        (L1_gnn_b_left, L1_gnn_b_right, L1_gnn_b_self, L1_gnn_gamma, L1_gnn_beta),
        (L2_gnn_bl[0], L2_gnn_br[0], L2_gnn_bs[0], L2_gnn_ln_w[0], L2_gnn_ln_b[0]),
        (L2_gnn_bl[1], L2_gnn_br[1], L2_gnn_bs[1], L2_gnn_ln_w[1], L2_gnn_ln_b[1]),
        (L3_gnn_bv, L3_gnn_bo),
    )
    weight_aps = [[give(f"weight{p}_{w}", np.asarray(m).T) for w, m in enumerate(ms)] for p, ms in enumerate(weights)]
    vector_aps = [[give(f"vector{p}_{v}", np.asarray(m)) for v, m in enumerate(vs)] for p, vs in enumerate(vectors)]
    x_ap, adj_ap, consts_ap = give("x_in", x), give("adj_in", adj), give("consts_in", consts)
    out = nc.dram_tensor("y_out", (GRAPHS, NODES, FEATURES), F32, kind="ExternalOutput").ap()
    build(nc, x_ap, adj_ap, consts_ap, weight_aps, vector_aps, out)
    return run_bass_kernel_spmd(nc, [arrays], core_ids=[0]).results[0]["y_out"]
```
